# Optimizing a Trainium2 kernel written in Bass

```python
import numpy as np
import jax
import jax.numpy as jnp

def _softmax(x, axis=-1):
    return jax.nn.softmax(x, axis=axis)

def _gelu(x):
    return jax.nn.gelu(x, approximate=True)

def _silu(x):
    return jax.nn.silu(x)

def _sigmoid(x):
    return jax.nn.sigmoid(x)

def _layernorm(x, axis=-1, eps=1e-05):
    m = jnp.mean(x, axis=axis, keepdims=True)
    v = jnp.var(x, axis=axis, keepdims=True)
    return (x - m) / jnp.sqrt(v + eps)

def _scatter_add(tgt, idx, src, axis=0):
    return tgt.at[idx].add(src)

def _segment_sum(src, seg, n):
    return jax.ops.segment_sum(src, seg, n)
kernel_name = 'mk_gnn_preln_d4_gnn_r32_6b5ea5'

def setup_inputs(seed: int=0):
    np.random.seed(seed)
    _w = jnp.asarray

    def _rec_inputs():
        import jax
        import jax.numpy as jnp
        _gk = jax.random.key(seed)
        x = -0.0001126 + 1 * jax.random.normal(jax.random.fold_in(_gk, 1), (3125, 256), jnp.float32)
        src = jax.random.randint(jax.random.fold_in(_gk, 2), (50000,), 0, 3125, jnp.int32)
        dst = jax.random.randint(jax.random.fold_in(_gk, 3), (50000,), 0, 3125, jnp.int32)
        _o = jnp.argsort(dst, stable=True)
        src = src[_o]
        dst = dst[_o]
        edge_weight = jax.random.uniform(jax.random.fold_in(_gk, 13), (50000,), jnp.float32, 0.0, 0.999999)
        return (x, src, dst, edge_weight)
    x, src, dst, edge_weight = _rec_inputs()

    def _L0_gnn_setup():
        import jax, jax.numpy as jnp
        import numpy as np
        N, IN_CH, HID, HEADS, OUT_CH, E = (30000, 256, 128, 4, 256, 15000)
        NEG_SLOPE = 0.2

        def gat_conv(x, W, a_src, a_dst, bias, src, dst, heads, out_ch, concat):
            n = x.shape[0]
            h = (x @ W).reshape(n, heads, out_ch)
            al_s = jnp.einsum('nhc,hc->nh', h, a_src)
            al_d = jnp.einsum('nhc,hc->nh', h, a_dst)
            logits = jax.nn.leaky_relu(al_s[src] + al_d[dst], NEG_SLOPE)
            m = jax.lax.stop_gradient(jax.ops.segment_max(logits, dst, num_segments=n))
            e = jnp.exp(logits - m[dst])
            denom = jax.ops.segment_sum(e, dst, num_segments=n)
            alpha = e / denom[dst]
            msg = h[src] * alpha[:, :, None]
            out = jax.ops.segment_sum(msg, dst, num_segments=n)
            out = out.reshape(n, heads * out_ch) if concat else out.mean(axis=1)
            return out + bias
        key = jax.random.key(seed)
        ks = jax.random.split(key, 12)
        s = lambda fin: 1.0 / np.sqrt(fin)
        return {'x': jax.random.normal(ks[0], (N, IN_CH), jnp.float32), 'edge_index': jax.random.randint(ks[1], (2, E), 0, N, jnp.int32), 'W1': jax.random.normal(ks[2], (IN_CH, HEADS * HID), jnp.float32) * s(IN_CH), 'a_src1': jax.random.normal(ks[3], (HEADS, HID), jnp.float32) * s(HID), 'a_dst1': jax.random.normal(ks[4], (HEADS, HID), jnp.float32) * s(HID), 'b1': jnp.zeros((HEADS * HID,), jnp.float32), 'prelu_w': jnp.asarray(0.25, jnp.float32), 'W2': jax.random.normal(ks[5], (HEADS * HID, OUT_CH), jnp.float32) * s(HEADS * HID), 'a_src2': jax.random.normal(ks[6], (1, OUT_CH), jnp.float32) * s(OUT_CH), 'a_dst2': jax.random.normal(ks[7], (1, OUT_CH), jnp.float32) * s(OUT_CH), 'b2': jnp.zeros((OUT_CH,), jnp.float32)}
    _L0_gnn_all = _L0_gnn_setup()
    _L0_gnn_in = {k: v for k, v in _L0_gnn_all.items() if k in ('W1', 'a_src1', 'a_dst1', 'b1', 'prelu_w', 'W2', 'a_src2', 'a_dst2', 'b2')}
    del _L0_gnn_all

    def _L1_gnn_setup():
        import jax, jax.numpy as jnp
        import numpy as np
        N_NODES = 50000
        IN_DIM = 256
        OUT_DIM = 128
        NUM_HEADS = 2
        N_EDGES = 25000

        def _gat_forward(x, edge_index, W_w, W_b, a):
            N = x.shape[0]
            H, D = (NUM_HEADS, OUT_DIM)
            Wh = (x @ W_w + W_b).reshape(N, H, D)
            src, dst = (edge_index[0], edge_index[1])
            a_src, a_dst = (a[:D], a[D:])
            s = jnp.einsum('nhd,d->nh', Wh, a_src)
            t = jnp.einsum('nhd,d->nh', Wh, a_dst)
            e = jax.nn.leaky_relu(s[src] + t[dst], negative_slope=0.2)
            m = jax.ops.segment_max(e, src, num_segments=N)
            ex = jnp.exp(e - m[src])
            denom = jax.ops.segment_sum(ex, src, num_segments=N)
            alpha = ex / denom[src]
            agg = jax.ops.segment_sum(alpha[:, :, None] * Wh[dst], src, num_segments=N)
            deg = jax.ops.segment_sum(jnp.ones_like(src, dtype=Wh.dtype), src, num_segments=N)
            h_prime = jnp.where(deg[:, None, None] > 0, agg, Wh)
            return h_prime.reshape(N, H * D)
        key = jax.random.key(seed)
        k1, k2, k3, k4, k5 = jax.random.split(key, 5)
        x = jax.random.normal(k1, (N_NODES, IN_DIM), dtype=jnp.float32)
        edge_index = jax.random.randint(k2, (2, N_EDGES), 0, N_NODES, dtype=jnp.int64)
        fan = IN_DIM + OUT_DIM * NUM_HEADS
        W_w = jax.random.uniform(k3, (IN_DIM, OUT_DIM * NUM_HEADS), dtype=jnp.float32, minval=-np.sqrt(6.0 / fan), maxval=np.sqrt(6.0 / fan))
        W_b = jnp.zeros((OUT_DIM * NUM_HEADS,), dtype=jnp.float32)
        fa = 1 + 2 * OUT_DIM
        a = jax.random.uniform(k4, (2 * OUT_DIM,), dtype=jnp.float32, minval=-np.sqrt(6.0 / fa), maxval=np.sqrt(6.0 / fa))
        return {'x': x, 'edge_index': edge_index, 'W_w': W_w, 'W_b': W_b, 'a': a}
    _L1_gnn_all = _L1_gnn_setup()
    _L1_gnn_in = {k: v for k, v in _L1_gnn_all.items() if k in ('W_w', 'W_b', 'a')}
    del _L1_gnn_all

    def _L2_gnn_setup():
        import jax, jax.numpy as jnp
        import numpy as np
        N_NODES = 50000
        N_EDGES = 50000
        D = 256

        def gcn_layer(x, row, col, w, W, b, n):
            x = x @ W
            deg = jax.ops.segment_sum(w, col, num_segments=n)
            dinv = jnp.where(deg > 0, jax.lax.rsqrt(deg), jnp.zeros((), x.dtype))
            norm = dinv[row] * w * dinv[col]
            out = jax.ops.segment_sum(norm[:, None] * x[row], col, num_segments=n)
            return out + b
        key = jax.random.key(seed)
        ks = jax.random.split(key, 6)
        X = jax.random.normal(ks[0], (N_NODES, D), dtype=jnp.float32)
        edge_index = jax.random.randint(ks[1], (2, N_EDGES), 0, N_NODES, dtype=jnp.int64)
        edge_weight = jax.random.uniform(ks[2], (N_EDGES,), dtype=jnp.float32)
        scale = 1.0 / np.sqrt(D)
        W1 = jax.random.normal(ks[3], (D, D), dtype=jnp.float32) * scale
        b1 = jnp.zeros((D,), dtype=jnp.float32)
        W2 = jax.random.normal(ks[4], (D, D), dtype=jnp.float32) * scale
        b2 = jnp.zeros((D,), dtype=jnp.float32)
        return {'X': X, 'edge_index': edge_index, 'edge_weight': edge_weight, 'W1': W1, 'b1': b1, 'W2': W2, 'b2': b2}
    _L2_gnn_all = _L2_gnn_setup()
    _L2_gnn_in = {k: v for k, v in _L2_gnn_all.items() if k in ('W1', 'b1', 'W2', 'b2')}
    del _L2_gnn_all

    def _L3_gnn_setup():
        import jax, jax.numpy as jnp
        import numpy as np
        N_NODES = 10000
        N_EDGES = 10000
        D = 256
        key = jax.random.key(seed)
        k1, k2, k3, k4, k5 = jax.random.split(key, 5)
        x = jax.random.normal(k1, (N_NODES, D), dtype=jnp.float32)
        src = jax.random.randint(k2, (N_EDGES,), 0, N_NODES, dtype=jnp.int32)
        dst = jax.random.randint(k3, (N_EDGES,), 0, N_NODES, dtype=jnp.int32)
        s = 1.0 / np.sqrt(D)
        theta_w = jax.random.uniform(k4, (D, D), jnp.float32, -s, s)
        theta_b = jnp.zeros((D,), jnp.float32)
        phi_w = jax.random.uniform(k5, (D, D), jnp.float32, -s, s)
        phi_b = jnp.zeros((D,), jnp.float32)
        return {'x': x, 'src': src, 'dst': dst, 'theta_w': theta_w, 'theta_b': theta_b, 'phi_w': phi_w, 'phi_b': phi_b}
    _L3_gnn_all = _L3_gnn_setup()
    _L3_gnn_in = {k: v for k, v in _L3_gnn_all.items() if k in ('theta_w', 'theta_b', 'phi_w', 'phi_b')}
    del _L3_gnn_all
    return {'x': x, 'src': src, 'dst': dst, 'edge_weight': edge_weight, 'L0_gnn_W1': _L0_gnn_in['W1'], 'L0_gnn_a_src1': _L0_gnn_in['a_src1'], 'L0_gnn_a_dst1': _L0_gnn_in['a_dst1'], 'L0_gnn_b1': _L0_gnn_in['b1'], 'L0_gnn_prelu_w': _L0_gnn_in['prelu_w'], 'L0_gnn_W2': _L0_gnn_in['W2'], 'L0_gnn_a_src2': _L0_gnn_in['a_src2'], 'L0_gnn_a_dst2': _L0_gnn_in['a_dst2'], 'L0_gnn_b2': _L0_gnn_in['b2'], 'L1_gnn_W_w': _L1_gnn_in['W_w'], 'L1_gnn_W_b': _L1_gnn_in['W_b'], 'L1_gnn_a': _L1_gnn_in['a'], 'L2_gnn_W1': _L2_gnn_in['W1'], 'L2_gnn_b1': _L2_gnn_in['b1'], 'L2_gnn_W2': _L2_gnn_in['W2'], 'L2_gnn_b2': _L2_gnn_in['b2'], 'L3_gnn_theta_w': _L3_gnn_in['theta_w'], 'L3_gnn_theta_b': _L3_gnn_in['theta_b'], 'L3_gnn_phi_w': _L3_gnn_in['phi_w'], 'L3_gnn_phi_b': _L3_gnn_in['phi_b']}

def reference(x, src, dst, edge_weight, L0_gnn_W1, L0_gnn_a_src1, L0_gnn_a_dst1, L0_gnn_b1, L0_gnn_prelu_w, L0_gnn_W2, L0_gnn_a_src2, L0_gnn_a_dst2, L0_gnn_b2, L1_gnn_W_w, L1_gnn_W_b, L1_gnn_a, L2_gnn_W1, L2_gnn_b1, L2_gnn_W2, L2_gnn_b2, L3_gnn_theta_w, L3_gnn_theta_b, L3_gnn_phi_w, L3_gnn_phi_b):
    import jax
    import jax.numpy as jnp

    def _L0_gnn_ref(x, edge_index, W1, a_src1, a_dst1, b1, prelu_w, W2, a_src2, a_dst2, b2):
        import jax, jax.numpy as jnp
        import numpy as np
        N, IN_CH, HID, HEADS, OUT_CH, E = (30000, 256, 128, 4, 256, 15000)
        NEG_SLOPE = 0.2

        def gat_conv(x, W, a_src, a_dst, bias, src, dst, heads, out_ch, concat):
            n = x.shape[0]
            h = (x @ W).reshape(n, heads, out_ch)
            al_s = jnp.einsum('nhc,hc->nh', h, a_src)
            al_d = jnp.einsum('nhc,hc->nh', h, a_dst)
            logits = jax.nn.leaky_relu(al_s[src] + al_d[dst], NEG_SLOPE)
            m = jax.lax.stop_gradient(jax.ops.segment_max(logits, dst, num_segments=n))
            e = jnp.exp(logits - m[dst])
            denom = jax.ops.segment_sum(e, dst, num_segments=n)
            alpha = e / denom[dst]
            msg = h[src] * alpha[:, :, None]
            out = jax.ops.segment_sum(msg, dst, num_segments=n)
            out = out.reshape(n, heads * out_ch) if concat else out.mean(axis=1)
            return out + bias
        n = x.shape[0]
        loop = jnp.arange(n, dtype=edge_index.dtype)
        src = jnp.concatenate([edge_index[0], loop])
        dst = jnp.concatenate([edge_index[1], loop])
        h = gat_conv(x, W1, a_src1, a_dst1, b1, src, dst, HEADS, HID, concat=True)
        h = jnp.where(h >= 0, h, prelu_w * h)
        z = gat_conv(h, W2, a_src2, a_dst2, b2, src, dst, 1, OUT_CH, concat=False)
        return z

    def _L1_gnn_ref(x, edge_index, W_w, W_b, a):
        import jax, jax.numpy as jnp
        import numpy as np
        N_NODES = 50000
        IN_DIM = 256
        OUT_DIM = 128
        NUM_HEADS = 2
        N_EDGES = 25000

        def _gat_forward(x, edge_index, W_w, W_b, a):
            N = x.shape[0]
            H, D = (NUM_HEADS, OUT_DIM)
            Wh = (x @ W_w + W_b).reshape(N, H, D)
            src, dst = (edge_index[0], edge_index[1])
            a_src, a_dst = (a[:D], a[D:])
            s = jnp.einsum('nhd,d->nh', Wh, a_src)
            t = jnp.einsum('nhd,d->nh', Wh, a_dst)
            e = jax.nn.leaky_relu(s[src] + t[dst], negative_slope=0.2)
            m = jax.ops.segment_max(e, src, num_segments=N)
            ex = jnp.exp(e - m[src])
            denom = jax.ops.segment_sum(ex, src, num_segments=N)
            alpha = ex / denom[src]
            agg = jax.ops.segment_sum(alpha[:, :, None] * Wh[dst], src, num_segments=N)
            deg = jax.ops.segment_sum(jnp.ones_like(src, dtype=Wh.dtype), src, num_segments=N)
            h_prime = jnp.where(deg[:, None, None] > 0, agg, Wh)
            return h_prime.reshape(N, H * D)
        return _gat_forward(x, edge_index, W_w, W_b, a)

    def _L2_gnn_ref(X, edge_index, edge_weight, W1, b1, W2, b2):
        import jax, jax.numpy as jnp
        import numpy as np
        N_NODES = 50000
        N_EDGES = 50000
        D = 256

        def gcn_layer(x, row, col, w, W, b, n):
            x = x @ W
            deg = jax.ops.segment_sum(w, col, num_segments=n)
            dinv = jnp.where(deg > 0, jax.lax.rsqrt(deg), jnp.zeros((), x.dtype))
            norm = dinv[row] * w * dinv[col]
            out = jax.ops.segment_sum(norm[:, None] * x[row], col, num_segments=n)
            return out + b
        n = X.shape[0]
        loop = jnp.arange(n, dtype=edge_index.dtype)
        row = jnp.concatenate([edge_index[0], loop])
        col = jnp.concatenate([edge_index[1], loop])
        w = jnp.concatenate([edge_weight, jnp.ones((n,), X.dtype)])
        h = jax.nn.relu(gcn_layer(X, row, col, w, W1, b1, n))
        h = jax.nn.relu(gcn_layer(h, row, col, w, W2, b2, n))
        return h

    def _L3_gnn_ref(x, src, dst, theta_w, theta_b, phi_w, phi_b):
        import jax, jax.numpy as jnp
        import numpy as np
        N_NODES = 10000
        N_EDGES = 10000
        D = 256
        x_src = x[src]
        x_dst = x[dst]
        theta_x = (x_dst - x_src) @ theta_w.T + theta_b
        phi_x = x_src @ phi_w.T + phi_b
        e = jax.nn.relu(theta_x + phi_x)
        out = jax.ops.segment_max(e, dst, num_segments=x.shape[0])
        return jnp.where(jnp.isfinite(out), out, 0.0)
    edge_index = jnp.stack([src, dst])
    h = jnp.maximum(_layernorm(x, axis=-1), 0.0)
    x = x + _L0_gnn_ref(h, edge_index, L0_gnn_W1, L0_gnn_a_src1, L0_gnn_a_dst1, L0_gnn_b1, L0_gnn_prelu_w, L0_gnn_W2, L0_gnn_a_src2, L0_gnn_a_dst2, L0_gnn_b2)
    h = jnp.maximum(_layernorm(x, axis=-1), 0.0)
    x = x + _L1_gnn_ref(h, edge_index, L1_gnn_W_w, L1_gnn_W_b, L1_gnn_a)
    h = jnp.maximum(_layernorm(x, axis=-1), 0.0)
    x = x + _L2_gnn_ref(h, edge_index, edge_weight, L2_gnn_W1, L2_gnn_b1, L2_gnn_W2, L2_gnn_b2)
    h = jnp.maximum(_layernorm(x, axis=-1), 0.0)
    x = x + _L3_gnn_ref(h, src, dst, L3_gnn_theta_w, L3_gnn_theta_b, L3_gnn_phi_w, L3_gnn_phi_b)
    return x

_drawn_inputs = setup_inputs


def setup_inputs(seed=0):
    import zlib

    import numpy as np

    out = dict(_drawn_inputs(seed))
    spreads = {'L0_gnn_b1': (0.0, 0.1),
     'L0_gnn_b2': (0.0, 0.1),
     'L1_gnn_W_b': (0.0, 0.1),
     'L2_gnn_b1': (0.0, 0.1),
     'L2_gnn_b2': (0.0, 0.1),
     'L3_gnn_theta_b': (0.0, 0.1),
     'L3_gnn_phi_b': (0.0, 0.1)}
    factors = {'edge_weight': 11.665,
     'L0_gnn_a_src1': 3.951,
     'L0_gnn_a_dst1': 8.0,
     'L0_gnn_a_src2': 8.0,
     'L0_gnn_a_dst2': 46.861}
    for name, (base, spread) in spreads.items():
        noise = np.random.default_rng([zlib.crc32(name.encode()), seed]).standard_normal(out[name].shape)
        drawn = base * np.exp(spread * noise) if base else spread * noise
        out[name] = jnp.asarray(drawn.astype(out[name].dtype))
    for name, factor in factors.items():
        out[name] = (out[name] * factor).astype(out[name].dtype)
    return out
```

```python
from contextlib import ExitStack

import numpy as np
import concourse.bass as bass
from concourse import mybir

P = 128
ALU = mybir.AluOpType
ACT = mybir.ActivationFunctionType
AX = mybir.AxisListType
F32 = mybir.dt.float32
I32 = mybir.dt.int32
BF16 = mybir.dt.bfloat16

SLOTS = 32
GROUP = 4
NGROUP = SLOTS // GROUP
KEYS = 64
TILES_AT_ONCE = 17
BIG = float(1 << 23)
NEG = -1.0e30
LOWEST = -3.0e38
LN_EPS = 1e-5
SLOPE = 0.2
IN, OUT = 0, 1
HEADER = 8


class Named:
    pass


def kernel_shapes(N, E):
    s = Named()
    s.N, s.E = N, E
    s.NT = -(-N // P)
    s.ET = -(-E // P)
    s.PAD_ROW = s.NT * P
    s.ROWS = s.PAD_ROW + 2 * P
    s.MAX_ITEMS = -(-E // SLOTS) + s.NT
    return s


class Mem:

    def __init__(self, nc, ctx):
        self.nc, self.ctx = nc, ctx
        self.phase_sems = []

    def sb(self, name, shape, dt=F32):
        return self.ctx.enter_context(self.nc.sbuf_tensor(name, shape, dt))

    def ps(self, name, shape):
        return self.ctx.enter_context(self.nc.psum_tensor(name, shape, F32))

    def dram(self, name, shape, dt=F32):
        return self.nc.dram_tensor(name, shape, dt, kind="Internal").ap()

    def sem(self, name):
        s = self.nc.alloc_semaphore(name=name)
        self.phase_sems.append(s)
        return s

    def end_phase(self):
        self.nc.all_engine_barrier()
        self.nc.clear_and_free_semaphores(self.phase_sems)
        self.nc.all_engine_barrier()
        self.phase_sems = []


def bc(ap, axis, n):
    u = ap.unsqueeze(axis)
    shape = list(u.shape)
    shape[axis] = n
    return u.broadcast_to(shape)


def constants(nc, M, G):
    G.ident = M.sb("ident", [P, P])
    G.ones_bf = M.sb("ones_bf", [P, P], BF16)
    G.lower_bf = M.sb("lower_bf", [P, P], BF16)
    G.lower = M.sb("lower", [P, P])
    G.upper = M.sb("upper", [P, P])
    G.same_parity = M.sb("same_parity", [32, 32])
    G.iota_row = M.sb("iota_row", [P, P])
    G.iota_col = M.sb("iota_col", [P, 1])
    G.ids = M.sb("ids", [P, G.NT])
    G.one_row = M.sb("one_row", [1, P])
    G.sc_i = M.sb("sc_i", [32, 32], I32)
    G.sc_i2 = M.sb("sc_i2", [32, 32], I32)
    G.s_const = M.sem("s_const")
    with nc.Block() as block:

        @block.gpsimd
        def _(pool):
            pool.memset(G.ident[:, :], 0.0)
            pool.memset(G.lower[:, :], 1.0)
            pool.memset(G.upper[:, :], 1.0)
            pool.memset(G.ones_bf[:, :], 1.0)
            pool.memset(G.one_row[:, :], 1.0)
            pool.drain()
            pool.affine_select(out=G.ident[:, :], in_=G.ident[:, :], compare_op=ALU.not_equal, fill=1.0,
                               base=0, pattern=[[-1, P]], channel_multiplier=1)
            pool.affine_select(out=G.lower[:, :], in_=G.lower[:, :], compare_op=ALU.is_gt, fill=0.0,
                               base=0, pattern=[[1, P]], channel_multiplier=-1)
            pool.affine_select(out=G.upper[:, :], in_=G.upper[:, :], compare_op=ALU.is_gt, fill=0.0,
                               base=0, pattern=[[-1, P]], channel_multiplier=1)
            pool.iota(G.iota_row[:, :], pattern=[[1, P]], base=0, channel_multiplier=0,
                      allow_small_or_imprecise_dtypes=True)
            pool.iota(G.iota_col[:, :], pattern=[[1, 1]], base=0, channel_multiplier=1,
                      allow_small_or_imprecise_dtypes=True)
            pool.iota(G.ids[:, :], pattern=[[P, G.NT]], base=0, channel_multiplier=1,
                      allow_small_or_imprecise_dtypes=True)
            pool.iota(G.sc_i[:, :], pattern=[[1, 32]], base=64, channel_multiplier=-1)
            pool.drain().then_inc(G.s_const, 1)

        @block.vector
        def _(dve):
            dve.wait_ge(G.s_const, 1)
            dve.tensor_copy(G.lower_bf[:, :], G.lower[:, :])
            dve.tensor_scalar(G.sc_i2[:, :], G.sc_i[:, :], 1, None, ALU.bitwise_and)
            dve.drain()
            dve.tensor_scalar(G.same_parity[:, :], G.sc_i2[:, :], 0.0, None, ALU.is_equal)
            dve.drain()
            dve.tensor_tensor(G.same_parity[:, :], G.same_parity[:, :], G.lower[0:32, 0:32], ALU.mult)


def edge_keys(nc, M, G, arena, src, dst, edge_weight):
    ET, E = G.ET, G.E
    full = E // ET
    rest = E - full * ET
    G.key_i = [arena(f"key_i{k}", ET, I32) for k in (IN, OUT)]
    G.lo_i = [arena(f"lo_i{k}", ET, I32) for k in (IN, OUT)]
    G.key = [G.work[:, k * ET:(k + 1) * ET] for k in (IN, OUT)]
    G.hi = [G.work[:, (2 + k) * ET:(3 + k) * ET] for k in (IN, OUT)]
    G.lo = [arena(f"lo{k}", ET) for k in (IN, OUT)]
    G.w = G.work[:, 4 * ET:5 * ET]
    G.rowT = arena("rowT", 4 * 4 * P)
    G.key_rows = M.dram("key_rows", [4, ET * P])
    s_pad, s_load, s_key, s_tr, s_cp, s_row = (M.sem(x) for x in
                                               ("s_pad", "s_load", "s_key", "s_tr", "s_cp", "s_row"))
    PT = G.banks
    nblk = -(-ET // P)
    with nc.Block() as block:

        @block.sync
        def _(sp):
            sp.wait_ge(s_pad, 1)
            for dst_t, a in ((G.key_i[IN], dst), (G.key_i[OUT], src), (G.w[:, :], edge_weight)):
                sp.dma_start(dst_t[0:full, :], a[0:full * ET].rearrange("(p t) -> p t", t=ET)).then_inc(s_load, 16)
                sp.dma_start(dst_t[full:full + 1, 0:rest],
                             a[full * ET:E].rearrange("(p t) -> p t", p=1)).then_inc(s_load, 16)
            sp.wait_ge(s_cp, 4)
            for q in range(4):
                for j in range(nblk):
                    m = min(P, ET - j * P)
                    sp.dma_start(G.key_rows[q, j * P * P:(j * P + m) * P].rearrange("(t p) -> t p", p=P),
                                 G.rowT[0:m, (q * 4 + j) * P:(q * 4 + j + 1) * P]).then_inc(s_row, 16)
            sp.wait_ge(s_row, 16 * 4 * nblk)

        @block.vector
        def _(dve):
            for k in (IN, OUT):
                dve.memset(G.key_i[k], G.PAD_ROW)
            dve.memset(G.w[:, :], 0.0)
            dve.drain().then_inc(s_pad, 1)
            dve.wait_ge(s_load, 96)
            for k in (IN, OUT):
                dve.tensor_scalar(G.lo_i[k], G.key_i[k], P - 1, None, ALU.bitwise_and)
                dve.tensor_copy(G.key[k][:, :], G.key_i[k])
            dve.drain()
            for k in (IN, OUT):
                dve.tensor_copy(G.lo[k], G.lo_i[k])
            dve.drain()
            for k in (IN, OUT):
                dve.tensor_tensor(G.hi[k][:, :], G.key[k][:, :], G.lo[k], ALU.subtract)
            dve.drain().then_inc(s_key, 1)
            for k in (IN, OUT):
                dve.tensor_scalar(G.hi[k][:, :], G.hi[k][:, :], 1.0 / P, None, ALU.mult)
            for q in range(4):
                dve.wait_ge(s_tr, q + 1)
                wide, m = (nblk - 1) * P, ET - (nblk - 1) * P
                dve.tensor_copy(G.rowT[:, q * 512:q * 512 + wide], PT[q][:, 0:wide])
                dve.tensor_copy(G.rowT[0:m, q * 512 + wide:(q + 1) * 512],
                                PT[q][0:m, wide:wide + P]).then_inc(s_cp, 1)

        @block.tensor
        def _(pe):
            pe.wait_ge(s_key, 1)
            for q, a in enumerate((G.key[IN][:, :], G.key[OUT][:, :], G.lo[IN], G.lo[OUT])):
                for j in range(nblk):
                    m = min(P, ET - j * P)
                    mm = pe.transpose(PT[q][0:m, j * P:(j + 1) * P], a[:, j * P:j * P + m], G.ident[:, :])
                mm.then_inc(s_tr, 1)


def histograms(nc, M, G, arena):
    TA, NT, ET = TILES_AT_ONCE, G.NT, G.ET
    steps = ET // TA
    assert steps * TA == ET and (TA + 1) * NT <= 512
    G.degree = [M.sb(f"degree{k}", [P, NT]) for k in (IN, OUT)]
    lo_hot = [arena(f"lo_hot{k}", TA * P // 2, BF16).rearrange("p (t b) -> p t b", t=TA) for k in (IN, OUT)]
    hi_hot = [arena(f"hi_hot{k}", TA * 26 // 2, BF16)[:, 0:TA * NT].rearrange("p (t a) -> p t a", t=TA)
              for k in (IN, OUT)]
    before = [b.rearrange("p (t a) -> p t a", a=NT) for b in G.before]
    s_hot, s_sum, s_read = ([M.sem(f"{x}{k}") for k in (IN, OUT)] for x in ("s_hot", "s_sum", "s_hread"))
    with nc.Block() as block:

        @block.vector
        def _(dve):
            for k in (IN, OUT):
                dve.memset(G.degree[k][:, :], 0.0)
            with dve.Fori(0, steps) as i:
                for k in (IN, OUT):
                    dve.wait_ge(s_sum[k], i + 1)
                    dve.tensor_tensor(lo_hot[k], bc(G.iota_row[:, :], 1, TA),
                                      bc(G.lo[k][:, bass.ts(i, TA)], 2, P), ALU.is_equal)
                    dve.tensor_tensor(hi_hot[k], bc(G.iota_row[:, 0:NT], 1, TA),
                                      bc(G.hi[k][:, bass.ts(i, TA)], 2, NT), ALU.is_equal).then_inc(s_hot[k], 1)
                for k in (IN, OUT):
                    dve.wait_ge(s_sum[k], i + 2)
                    sums = G.banks[k][:, 0:(TA + 1) * NT].rearrange("p (t a) -> p t a", a=NT)
                    at = before[k][:, bass.ts(i, TA), :]
                    dve.tensor_copy(at[:, 0, :], G.degree[k][:, :])
                    dve.tensor_tensor(at[:, 1:TA, :], sums[:, 1:TA, :], bc(G.degree[k][:, :], 1, TA - 1), ALU.add)
                    dve.drain()
                    dve.tensor_tensor(G.degree[k][:, :], G.degree[k][:, :], sums[:, TA, :],
                                      ALU.add).then_inc(s_read[k], 1)
                    dve.drain()

        @block.tensor
        def _(pe):
            for k in (IN, OUT):
                pe.sem_inc(s_sum[k], 1)
            with pe.Fori(0, steps) as i:
                for k in (IN, OUT):
                    pe.wait_ge(s_hot[k], i + 1)
                    pe.wait_ge(s_read[k], i + 1)
                    for j in range(TA):
                        mm = pe.matmul(G.banks[k][:, (j + 1) * NT:(TA + 1) * NT].rearrange("p (t a) -> p t a", a=NT),
                                       lhsT=lo_hot[k][:, j, :], rhs=bc(hi_hot[k][:, j, :], 1, TA - j),
                                       start=(j == 0), stop=(j == TA - 1), skip_group_check=True)
                    mm.then_inc(s_sum[k], 1)

        @block.sync
        def _(sp):
            for k in (IN, OUT):
                sp.sem_inc(s_read[k], 1)


def node_order(nc, M, G, arena):
    NT = G.NT
    AG = 5
    assert NT % AG == 0 and AG * KEYS <= 512
    cls = arena("cls", NT)
    hot = arena("cls_hot", NT * KEYS // 2, BF16).rearrange("p (a k) -> p a k", k=KEYS)
    cum = arena("cls_cum", (NT + 1) * KEYS // 2, BF16).rearrange("p (a k) -> p a k", k=KEYS)
    count = arena("cls_count", KEYS)
    suf = [arena(f"suf{j}", KEYS) for j in range(2)]
    rank = arena("rank", NT * KEYS).rearrange("p (a k) -> p a k", k=KEYS)
    G.base_pos = M.sb("base_pos", [P, 2, 2, NT])
    G.pos_i = M.sb("pos_i", [P, NT], I32)
    meta = arena("meta", NT * 4).rearrange("p (a q) -> p a q", q=4)
    G.meta = M.dram("meta", [G.PAD_ROW, 4])
    G.by_pos = M.sb("by_pos", [P, NT, 4])
    G.bounds_dram = M.dram("bounds_dram", [2, 32 * HEADER], I32)
    G.bounds = [M.sb(f"bounds{k}", [1, 32 * HEADER], I32) for k in (IN, OUT)]
    G.ids_i = M.sb("ids_i", [P, NT], I32)
    G.ids_in = M.sb("ids_in", [P, NT], I32)
    t_i = arena("t_i", 64, I32)
    t2_i = arena("t2_i", 64, I32)
    bnd = [arena(f"bnd{k}", HEADER) for k in (IN, OUT)]
    bnd_i = [arena(f"bnd_i{k}", HEADER, I32) for k in (IN, OUT)]
    kmax = arena("kmax", 2)
    tile_i = arena("tile_i", NT, I32)
    low_i = arena("low_i", NT, I32)
    tile_f = arena("tile_f", NT)
    low_f = arena("low_f", NT)
    tile_hot = arena("tile_hot", NT * NT).rearrange("p (a n) -> p a n", n=NT)
    picked = arena("picked", NT * NT).rearrange("p (a n) -> p a n", n=NT)
    first = [arena(f"first{k}", 32 * HEADER, I32) for k in (IN, OUT)]
    first_f = [arena(f"first_f{k}", NT) for k in (IN, OUT)]
    s_o = Named()
    s_o.hot = M.sem("s_o_hot")
    s_o.cum = M.sem("s_o_cum")
    s_o.count = M.sem("s_o_count")
    s_o.rank = M.sem("s_o_rank")
    s_o.read = M.sem("s_o_read")
    s_o.pos = M.sem("s_o_pos")
    s_o.meta = M.sem("s_o_meta")
    s_o.load = M.sem("s_o_load")
    s_o.tr = M.sem("s_o_tr")
    s_o.max = M.sem("s_o_max")
    s_o.cum2 = M.sem("s_o_cum2")
    s_o.bnd = M.sem("s_o_bnd")
    s_o.bst = M.sem("s_o_bst")
    s_o.bld = M.sem("s_o_bld")
    with nc.Block() as block:

        @block.vector
        def _(dve):
            dve.tensor_scalar(cls, G.degree[IN][:, :], float(KEYS - 1), None, ALU.min)
            dve.drain()
            dve.tensor_tensor(hot, bc(G.iota_row[:, 0:KEYS], 1, NT), bc(cls, 2, KEYS), ALU.is_equal)
            dve.memset(cum[:, 0, :], 0.0)
            dve.drain()
            for a in range(NT):
                dve.tensor_tensor(cum[:, a + 1, :], cum[:, a, :], hot[:, a, :], ALU.add)
                dve.drain()
            dve.drain().then_inc(s_o.hot, 1)
            dve.wait_ge(s_o.count, 1)
            dve.tensor_copy(count, G.banks[5][:, 0:KEYS])
            dve.drain()
            dve.tensor_copy(suf[0], count)
            dve.drain()
            cur, step = 0, 1
            while step < KEYS:
                dve.tensor_tensor(suf[1 - cur][:, 0:KEYS - step], suf[cur][:, 0:KEYS - step],
                                  suf[cur][:, step:KEYS], ALU.add)
                dve.tensor_copy(suf[1 - cur][:, KEYS - step:KEYS], suf[cur][:, KEYS - step:KEYS])
                dve.drain()
                cur, step = 1 - cur, 2 * step
            dve.tensor_tensor(count, suf[cur], count, ALU.subtract)
            dve.drain()
            dve.wait_ge(s_o.rank, NT // AG)
            for g in range(NT // AG):
                dve.tensor_tensor(rank[:, g * AG:(g + 1) * AG, :],
                                  G.banks[g][:, 0:AG * KEYS].rearrange("p (a k) -> p a k", k=KEYS),
                                  bc(count, 1, AG), ALU.add)
            dve.drain()
            dve.tensor_tensor(rank, rank, hot, ALU.mult)
            dve.drain()
            for k in (IN, OUT):
                dve.tensor_reduce(G.base_pos[:, k, 1, :], rank, AX.X, ALU.add)
            dve.drain()
            dve.tensor_copy(G.pos_i[:, :], G.base_pos[:, IN, 1, :])
            dve.tensor_copy(meta[:, :, 0], G.ids[:, :])
            dve.tensor_copy(meta[:, :, 1], G.degree[IN][:, :])
            dve.tensor_copy(meta[:, :, 2], G.degree[OUT][:, :])
            dve.memset(meta[:, :, 3], 0.0)
            dve.drain().then_inc(s_o.pos, 1)
            dve.tensor_scalar(tile_i, G.pos_i[:, :], 7, None, ALU.logical_shift_right)
            dve.tensor_scalar(low_i, G.pos_i[:, :], P - 1, None, ALU.bitwise_and)
            dve.drain()
            dve.tensor_copy(tile_f, tile_i)
            dve.tensor_copy(low_f, low_i)
            dve.drain()
            dve.tensor_tensor(tile_hot, bc(G.iota_row[:, 0:NT], 1, NT), bc(tile_f, 2, NT), ALU.is_equal)
            dve.wait_ge(s_o.load, 16)
            dve.tensor_copy(G.ids_i[:, :], G.by_pos[:, :, 0])
            dve.tensor_scalar(G.ids_in[:, :], G.by_pos[:, :, 0], float(G.N - 1), None, ALU.min)
            dve.wait_ge(s_o.tr, 1)
            for k in (IN, OUT):
                dve.tensor_reduce(kmax[0:NT, k:k + 1], G.banks[6][0:NT, k * P:(k + 1) * P], AX.X, ALU.max)
            dve.drain()
            for k in (IN, OUT):
                dve.memset(bnd[k][0:32, :], 0.0)
                dve.tensor_scalar(kmax[0:NT, k:k + 1], kmax[0:NT, k:k + 1], 1.0, None, ALU.max)
            dve.drain()
            for k in (IN, OUT):
                dve.tensor_copy(bnd[k][0:NT, 0:1], kmax[0:NT, k:k + 1])
                dve.tensor_scalar(t_i[0:NT, 2 * k:2 * k + 1], kmax[0:NT, k:k + 1], float(SLOTS - 1), None, ALU.add)
                dve.tensor_scalar(t_i[0:NT, 2 * k + 1:2 * k + 2], kmax[0:NT, k:k + 1], float(GROUP - 1), None, ALU.add)
            dve.drain()
            for k in (IN, OUT):
                dve.tensor_scalar(t2_i[0:NT, 2 * k:2 * k + 1], t_i[0:NT, 2 * k:2 * k + 1], 5, None,
                                  ALU.logical_shift_right)
                dve.tensor_scalar(t2_i[0:NT, 2 * k + 1:2 * k + 2], t_i[0:NT, 2 * k + 1:2 * k + 2], 2, None,
                                  ALU.logical_shift_right)
            dve.drain()
            for k in (IN, OUT):
                dve.tensor_scalar(t_i[0:NT, 2 * k:2 * k + 1], kmax[0:NT, k:k + 1], 1.0, None, ALU.add)
            dve.drain()
            for k in (IN, OUT):
                dve.tensor_scalar(t_i[0:NT, 2 * k + 1:2 * k + 2], t_i[0:NT, 2 * k:2 * k + 1], 1, None,
                                  ALU.logical_shift_right)
            dve.drain()
            for k in (IN, OUT):
                dve.tensor_scalar(bnd[k][0:NT, 6:7], t_i[0:NT, 2 * k + 1:2 * k + 2], 2.0, None, ALU.mult)
                dve.tensor_scalar(bnd[k][0:NT, 7:8], t2_i[0:NT, 2 * k + 1:2 * k + 2], float(GROUP), None, ALU.mult)
                dve.tensor_copy(bnd[k][0:NT, 1:2], t2_i[0:NT, 2 * k:2 * k + 1])
                dve.tensor_copy(bnd[k][0:NT, 5:6], t2_i[0:NT, 2 * k + 1:2 * k + 2])
            dve.drain().then_inc(s_o.max, 1)
            dve.wait_ge(s_o.cum2, 1)
            for k in (IN, OUT):
                for col, q in ((2, 0), (4, 1), (3, 2), (6, 3), (7, 4)):
                    dve.tensor_copy(bnd[k][0:32, col:col + 1], G.banks[7][0:32, 8 * k + q:8 * k + q + 1])
            dve.drain()
            for k in (IN, OUT):
                dve.tensor_copy(bnd_i[k][0:32, :], bnd[k][0:32, :])
            dve.drain().then_inc(s_o.bnd, 1)
            dve.wait_ge(s_o.bld, 64)
            for k in (IN, OUT):
                dve.tensor_copy(first_f[k], first[k][:, 0:NT * HEADER].rearrange("p (n h) -> p n h", h=HEADER)[:, :, 2])
            dve.drain()
            for k in (IN, OUT):
                dve.tensor_tensor(picked, tile_hot, bc(first_f[k], 1, NT), ALU.mult)
                dve.drain()
                dve.tensor_reduce(G.base_pos[:, k, 0, :], picked, AX.X, ALU.add)
                dve.drain()
                dve.tensor_scalar(G.base_pos[:, k, 0, :], G.base_pos[:, k, 0, :], float(P), None, ALU.mult)
                dve.drain()
                dve.tensor_tensor(G.base_pos[:, k, 0, :], G.base_pos[:, k, 0, :], low_f, ALU.add)
                dve.drain()
                dve.tensor_scalar(G.base_pos[:, k, 0, :], G.base_pos[:, k, 0, :], float(SLOTS), None, ALU.mult)
                dve.drain()

        @block.tensor
        def _(pe):
            pe.wait_ge(s_o.hot, 1)
            pe.matmul(G.banks[5][:, 0:KEYS], lhsT=G.ones_bf[:, :], rhs=cum[:, NT, :],
                      start=True, stop=True).then_inc(s_o.count, 1)
            for g in range(NT // AG):
                out = G.banks[g][:, 0:AG * KEYS].rearrange("p (a k) -> p a k", k=KEYS)
                pe.matmul(out, lhsT=G.lower_bf[:, :], rhs=hot[:, g * AG:(g + 1) * AG, :], start=True, stop=False)
                pe.matmul(out, lhsT=G.ones_bf[:, :], rhs=cum[:, g * AG:(g + 1) * AG, :],
                          start=False, stop=True).then_inc(s_o.rank, 1)
            pe.wait_ge(s_o.load, 16)
            pe.transpose(G.banks[6][0:NT, 0:P], G.by_pos[:, :, 1], G.ident[:, :])
            pe.transpose(G.banks[6][0:NT, P:2 * P], G.by_pos[:, :, 2], G.ident[:, :]).then_inc(s_o.tr, 1)
            pe.wait_ge(s_o.max, 1)
            for k in (IN, OUT):
                for q, (mask, col) in enumerate(((G.lower, 1), (G.lower, 5), (G.same_parity, 1), (G.same_parity, 6),
                                                 (G.same_parity, 7))):
                    mm = pe.matmul(G.banks[7][0:32, 8 * k + q:8 * k + q + 1], lhsT=mask[0:NT, 0:32],
                                   rhs=bnd[k][0:NT, col:col + 1], start=(k == IN and q == 0), stop=True,
                                   skip_group_check=True)
            mm.then_inc(s_o.cum2, 1)

        @block.gpsimd
        def _(pool):
            pool.wait_ge(s_o.pos, 1)
            for a in range(NT):
                pool.indirect_dma_start(out=G.meta[:, :], out_offset=bass.IndirectOffsetOnAxis(
                    ap=G.pos_i[:, a:a + 1], axis=0), in_=meta[:, a, :], in_offset=None).then_inc(s_o.meta, 16)

        @block.sync
        def _(sp):
            sp.wait_ge(s_o.meta, 16 * NT)
            sp.dma_start(G.by_pos[:, :, :], G.meta.rearrange("(n p) q -> p n q", p=P)).then_inc(s_o.load, 16)
            sp.wait_ge(s_o.bnd, 1)
            for k in (IN, OUT):
                sp.dma_start(G.bounds_dram[k].rearrange("(n h) -> n h", h=HEADER), bnd_i[k][0:32, :]).then_inc(s_o.bst, 16)
            sp.wait_ge(s_o.bst, 32)
            for k in (IN, OUT):
                row = G.bounds_dram[k].rearrange("(o n) -> o n", o=1)
                sp.dma_start(G.bounds[k][:, :], row).then_inc(s_o.bld, 16)
                sp.dma_start(first[k], row.broadcast_to([P, 32 * HEADER])).then_inc(s_o.bld, 16)
            sp.wait_ge(s_o.bld, 64)


def scatter_edges(nc, M, G, arena):
    TA, NT, ET = TILES_AT_ONCE, G.NT, G.ET
    steps = ET // TA
    per_bank = 6
    assert per_bank * 3 * NT <= 512 and -(-TA // per_bank) == 3
    rows = G.MAX_ITEMS * P * SLOTS
    G.lists = [M.dram(f"lists{k}", [2 * rows, 2], I32) for k in (IN, OUT)]
    before = [b.rearrange("p (t a) -> p t a", a=NT) for b in G.before]
    row = [[arena(f"row{x}{k}", TA * P) for k in (IN, OUT)] for x in ("key", "lo")]
    lo_hot = [arena("lo_hot_in", TA * P), G.early[:, 0:TA * P]]
    hi_hot = arena("hi_hot_f", TA * NT).rearrange("p (t a) -> p t a", a=NT)
    looked = arena("looked", TA * 3 * NT).rearrange("p (t q a) -> p t q a", q=3, a=NT)
    value = [arena(f"value{k}", TA * 3).rearrange("p (t q) -> p t q", q=3) for k in (IN, OUT)]
    inside = [arena(f"inside{k}", TA) for k in (IN, OUT)]
    number = arena("number", TA)
    number_i, chunk_i, slot_i = (arena(x, TA, I32) for x in ("number_i", "chunk_i", "slot_i"))
    chunk_f, slot_f = arena("chunk_f", TA), arena("slot_f", TA)
    out_f = [arena(f"out_f{k}", TA) for k in (IN, OUT)]
    address = [[M.sb(f"address{k}_{x}", [P, TA], I32) for k in (IN, OUT)] for x in range(2)]
    entry = [[M.sb(f"entry{k}_{x}", [P, TA, 2], I32) for k in (IN, OUT)] for x in range(2)]
    assert steps % 2 == 1
    empty = M.sb("empty", [P, SLOTS, 2], I32)
    s_e = Named()
    s_e.empty = M.sem("s_e_empty")
    s_e.fill = M.sem("s_e_fill")
    s_e.rows_free = M.sem("s_e_rows_free")
    s_e.hot = M.sem("s_e_hot")
    s_e.look = M.sem("s_e_look")
    s_e.lread = M.sem("s_e_lread")
    s_e.entry = M.sem("s_e_entry")
    s_e.sent = M.sem("s_e_sent")
    scatter = [M.sem(f"s_e_scatter{x}") for x in range(2)]
    s_e.filled = M.sem("s_e_filled")
    s_e.seen = M.sem("s_e_seen")
    s_rows = [M.sem(f"s_e_rows{x}{k}") for x in range(2) for k in (IN, OUT)]
    with nc.Block() as block:

        @block.sync
        def _(sp):
            sp.wait_ge(s_e.empty, 1)
            total = [sp.value_load(G.bounds[k][0:1, NT * HEADER + 2:NT * HEADER + 3], min_val=NT,
                                   max_val=G.MAX_ITEMS) for k in (IN, OUT)]
            for k in (IN, OUT):
                with sp.Fori(0, total[k]) as q:
                    sp.dma_start(G.lists[k].rearrange("(q p s) c -> q p (s c)", p=P, s=SLOTS)[bass.ds(q, 1)].rearrange(
                        "q p s -> (q p) s"), empty[:, :, :].rearrange("p s c -> p (s c)")).then_inc(s_e.fill, 16)
            sp.wait_ge(s_e.fill, (total[IN] + total[OUT]) * 16)
            sp.sem_inc(s_e.filled, 1)
            with sp.Fori(0, steps) as i:
                sp.wait_ge(s_e.rows_free, i + 1)
                for x in range(2):
                    for k in (IN, OUT):
                        sp.dma_start(row[x][k], G.key_rows[2 * x + k:2 * x + k + 1, bass.ds(i * (TA * P), TA * P)].broadcast_to(
                            [P, TA * P])).then_inc(s_rows[2 * x + k], 16)

        @block.vector
        def _(dve):
            dve.memset(empty[:, :, 0], G.PAD_ROW)
            dve.memset(empty[:, :, 1], 0)
            dve.drain().then_inc(s_e.empty, 1)
            dve.sem_inc(s_e.rows_free, 1)

            def step(i, x):
                for k in (IN, OUT):
                    dve.wait_ge(s_rows[2 + k], i * 16 + 16)
                    dve.wait_ge(s_e.look, i * 2 + (k + 1))
                    dve.tensor_scalar(lo_hot[k], row[1][k], G.iota_col[:, 0:1], None,
                                      ALU.is_equal).then_inc(s_e.hot, 1)
                for k in (IN, OUT):
                    dve.wait_ge(s_rows[k], i * 16 + 16)
                    for t in range(TA):
                        dve.scalar_tensor_tensor(out=row[0][k][:, t * P:(t + 1) * P], in0=row[0][k][:, t * P:(t + 1) * P],
                                                 scalar=G.key[k][:, bass.ds(i * TA + t, 1)], in1=G.upper[:, :],
                                                 op0=ALU.is_equal, op1=ALU.mult, accum_out=inside[k][:, t:t + 1])
                    dve.tensor_scalar(out_f[k], G.key[k][:, bass.ts(i, TA)], float(G.PAD_ROW), BIG,
                                      ALU.is_equal, ALU.mult)
                dve.drain()
                dve.sem_inc(s_e.rows_free, 1)
                for k in (IN, OUT):
                    dve.tensor_tensor(hi_hot, bc(G.iota_row[:, 0:NT], 1, TA),
                                      bc(G.hi[k][:, bass.ts(i, TA)], 2, NT), ALU.is_equal)
                    dve.drain()
                    dve.wait_ge(s_e.look, i * 2 + (k + 3))
                    for b in range(3):
                        n = min(per_bank, TA - b * per_bank)
                        got = G.banks[3 * k + b][:, 0:n * 3 * NT].rearrange("p (t q a) -> p t q a", q=3, a=NT)
                        for q in range(3):
                            ins = dve.tensor_tensor(looked[:, b * per_bank:b * per_bank + n, q, :], got[:, :, q, :],
                                                    hi_hot[:, b * per_bank:b * per_bank + n, :], ALU.mult)
                    ins.then_inc(s_e.lread, 1)
                    dve.drain()
                    dve.tensor_reduce(value[k], looked, AX.X, ALU.add)
                    dve.drain()
                    dve.tensor_tensor(number, value[k][:, :, 0], inside[k], ALU.add)
                    dve.drain()
                    dve.tensor_copy(number_i, number)
                    dve.drain()
                    dve.tensor_scalar(chunk_i, number_i, 5, None, ALU.logical_shift_right)
                    dve.tensor_scalar(slot_i, number_i, SLOTS - 1, None, ALU.bitwise_and)
                    dve.drain()
                    dve.tensor_copy(chunk_f, chunk_i)
                    dve.tensor_copy(slot_f, slot_i)
                    dve.drain()
                    dve.scalar_tensor_tensor(out=number, in0=chunk_f, scalar=float(P * SLOTS), in1=slot_f,
                                             op0=ALU.mult, op1=ALU.add)
                    dve.tensor_tensor(out_f[k], out_f[k], value[k][:, :, 1], ALU.add)
                    dve.drain()
                    if k == IN:
                        dve.wait_ge(s_e.sent, i + 1)
                    dve.tensor_tensor(address[x][k][:, :], number, out_f[k], ALU.add)
                    dve.drain()
                for k in (IN, OUT):
                    dve.tensor_copy(entry[x][k][:, :, 0], value[1 - k][:, :, 2])
                    dve.tensor_copy(entry[x][k][:, :, 1].bitcast(F32), G.w[:, bass.ts(i, TA)])
                dve.drain().then_inc(s_e.entry, 1)

            step(0, 0)
            with dve.Fori(0, steps // 2) as j:
                step(j * 2 + 1, 1)
                step(j * 2 + 2, 0)

        @block.tensor
        def _(pe):
            pe.sem_inc(s_e.look, 2)
            pe.sem_inc(s_e.lread, 2)
            with pe.Fori(0, steps) as i:
                for k in (IN, OUT):
                    pe.wait_ge(s_e.hot, i * 2 + (k + 1))
                    pe.wait_ge(s_e.lread, i * 2 + (k + 1))
                    for t in range(TA):
                        at = G.banks[3 * k + t // per_bank][:, (t % per_bank) * 3 * NT:(t % per_bank + 1) * 3 * NT]
                        pe.matmul(at[:, 0:NT], lhsT=lo_hot[k][:, t * P:(t + 1) * P],
                                  rhs=before[k][:, bass.ds(i * TA + t, 1), :].rearrange("p o a -> p (o a)"),
                                  start=(t % per_bank == 0), stop=True, skip_group_check=True)
                        mm = pe.matmul(at[:, NT:3 * NT], lhsT=lo_hot[k][:, t * P:(t + 1) * P],
                                       rhs=G.base_pos[:, k, :, :].rearrange("p q a -> p (q a)"),
                                       start=False, stop=True, skip_group_check=True)
                    mm.then_inc(s_e.look, 1)

        @block.gpsimd
        def _(pool):
            pool.sem_inc(s_e.sent, 2)
            pool.wait_ge(s_e.filled, 1)
            last_row = pool.to_reg(rows - 1)

            def step(i, x, j):
                pool.wait_ge(s_e.entry, i + 1)
                pool.sem_inc(s_e.seen, 1)
                for t in range(TA):
                    if t == TA // 2 and j is not None:
                        pool.wait_ge(scatter[1 - x], j * (2 * 16 * TA) + 2 * 16 * TA)
                        pool.sem_inc(s_e.sent, 1)
                    for k in (IN, OUT):
                        pool.indirect_dma_start(out=G.lists[k][:, :], out_offset=bass.IndirectOffsetOnAxis(
                            ap=address[x][k][:, t:t + 1], axis=0), in_=entry[x][k][:, t, :], in_offset=None,
                            bounds_check=last_row, oob_is_err=False).then_inc(scatter[x], 16)

            step(0, 0, None)
            with pool.Fori(0, steps // 2) as j:
                step(j * 2 + 1, 1, j)
                step(j * 2 + 2, 0, j)
            for x in range(2):
                pool.wait_ge(scatter[x], (steps + 1 - x) // 2 * 2 * 16 * TA)


def weights(nc, M, G, a):
    H1, C1 = 4, 128
    G.W1 = G.early[:, 0:2 * 520].rearrange("p (k n) -> p k n", k=2)
    G.W2 = G.early[:, 2 * 520:2 * 520 + 4 * 258].rearrange("p (k n) -> p k n", k=4)
    G.W3 = M.sb("W3", [P, 2, 260])
    G.W4 = M.sb("W4", [P, 2, 256])
    G.W5 = M.sb("W5", [P, 2, 256])
    G.W6 = M.sb("W6", [P, 2, 512])
    G.row3 = M.sb("row3", [1, 260])
    G.row6 = M.sb("row6", [1, 512])
    G.b1 = M.sb("b1", [P, 512])
    G.b2 = M.sb("b2", [P, 256])
    G.b4 = M.sb("b4", [P, 256])
    G.b5 = M.sb("b5", [P, 256])
    G.slope = M.sb("slope", [P, 1])
    store, at = G.store, [G.arena_at]

    def tmp(n):
        at[0] += n
        return store[:, at[0] - n:at[0]]

    as1, ad1, as2, ad2, a3 = tmp(512), tmp(512), tmp(256), tmp(256), tmp(256)
    th, ph = tmp(512).rearrange("p (k n) -> p k n", k=2), tmp(512).rearrange("p (k n) -> p k n", k=2)
    rb = tmp(512)
    junk = tmp(40 * 128).rearrange("p (j n) -> p j n", n=128)
    junk2 = tmp(8 * 256).rearrange("p (j n) -> p j n", n=256)
    zero, lowest = tmp(520), tmp(256)
    G.tables = [M.dram(f"table{j}", [G.ROWS, w]) for j, w in enumerate((520, 258, 260, 256, 256, 256))]
    G.own6 = M.dram("own6", [G.ROWS, 256])
    s_w, s_d, s_t, s_z, s_zd = M.sem("s_w"), M.sem("s_wd"), M.sem("s_wt"), M.sem("s_wz"), M.sem("s_wzd")

    def row(x):
        return x.rearrange("(o n) -> o n", o=1)

    with nc.Block() as block:

        @block.sync
        def _(sp):
            loads = [
                (G.W1[:, :, 0:512], a.W1.rearrange("(k p) n -> p k n", p=P)),
                (G.W2[:, :, 0:256], a.W2.rearrange("(k p) n -> p k n", p=P)),
                (G.W3[:, :, 0:256], a.W3.rearrange("(k p) n -> p k n", p=P)),
                (G.W4[:, :, :], a.W4.rearrange("(k p) n -> p k n", p=P)),
                (G.W5[:, :, :], a.W5.rearrange("(k p) n -> p k n", p=P)),
                (th, a.theta.rearrange("(k p) n -> p k n", p=P)),
                (ph, a.phi.rearrange("(k p) n -> p k n", p=P)),
                (as1, a.as1.rearrange("(o h) c -> o (h c)", o=1).broadcast_to([P, 512])),
                (ad1, a.ad1.rearrange("(o h) c -> o (h c)", o=1).broadcast_to([P, 512])),
                (as2, a.as2.broadcast_to([P, 256])),
                (ad2, a.ad2.broadcast_to([P, 256])),
                (a3, row(a.a3).broadcast_to([P, 256])),
                (G.b1[:, :], row(a.b1).broadcast_to([P, 512])),
                (G.b2[:, :], row(a.b2).broadcast_to([P, 256])),
                (G.b4[:, :], row(a.b4).broadcast_to([P, 256])),
                (G.b5[:, :], row(a.b5).broadcast_to([P, 256])),
                (G.slope[:, :], a.slope.broadcast_to([P, 1])),
                (G.row3[0:1, 0:256], row(a.b3)),
                (G.row6[0:1, 256:512], row(a.theta_b)),
                (rb[0:1, 0:256], row(a.phi_b)),
            ]
            for dst, src in loads:
                sp.dma_start(dst, src).then_inc(s_w, 16)
            sp.wait_ge(s_z, 1)
            for j, t in enumerate(G.tables):
                empty = lowest if j == len(G.tables) - 1 else zero
                sp.dma_start(t[G.PAD_ROW:G.PAD_ROW + 1, :], empty[0:1, 0:t.shape[1]]).then_inc(s_zd, 16)
            sp.wait_ge(s_zd, 16 * len(G.tables))
        NL = 20

        @block.vector
        def _(dve):
            dve.memset(zero[0:1, :], 0.0)
            dve.memset(lowest[0:1, :], LOWEST)
            dve.memset(G.row6[0:1, 0:256], 0.0)
            dve.drain().then_inc(s_z, 1)
            dve.wait_ge(s_w, 16 * NL)
            j = 0
            for k in range(2):
                for h in range(H1):
                    for v, vec in ((0, as1), (4, ad1)):
                        cols = slice(h * C1, (h + 1) * C1)
                        dve.tensor_tensor_reduce(junk[:, j, :], G.W1[:, k, cols], vec[:, cols], 1.0, 0.0,
                                                 ALU.mult, ALU.add, G.W1[:, k, 512 + v + h:513 + v + h])
                        j += 1
            for k in range(4):
                for v, vec in ((0, as2), (1, ad2)):
                    dve.tensor_tensor_reduce(junk2[:, 2 * k + v, :], G.W2[:, k, 0:256], vec, 1.0, 0.0,
                                             ALU.mult, ALU.add, G.W2[:, k, 256 + v:257 + v])
            for k in range(3):
                src, n = (G.W3[:, k, :], P) if k < 2 else (G.row3[:, :], 1)
                for h in range(2):
                    for v in range(2):
                        dve.tensor_tensor_reduce(junk[0:n, j, :], src[:, h * P:(h + 1) * P],
                                                 a3[0:n, (1 - v) * P:(2 - v) * P], 1.0, 0.0, ALU.mult, ALU.add,
                                                 src[:, 256 + 2 * v + h:257 + 2 * v + h])
                        j += 1
            dve.tensor_tensor(ph, ph, th, ALU.subtract)
            dve.tensor_tensor(G.row6[0:1, 256:512], G.row6[0:1, 256:512], rb[0:1, 0:256], ALU.add)
            dve.drain().then_inc(s_d, 1)
            dve.wait_ge(s_t, 1)
            for v in range(2):
                for k in range(2):
                    dve.tensor_copy(G.W6[:, k, v * 256:(v + 1) * 256],
                                    G.banks[v][:, k * 256:(k + 1) * 256])

        @block.tensor
        def _(pe):
            pe.wait_ge(s_d, 1)
            for v, x in enumerate((ph, th)):
                for k in range(2):
                    for o in range(2):
                        mm = pe.transpose(G.banks[v][:, k * 256 + o * P:k * 256 + (o + 1) * P],
                                          x[:, o, k * P:(k + 1) * P], G.ident[:, :])
            mm.then_inc(s_t, 1)


def first_rows(nc, M, G, x):
    G.x_all = G.store[:, 0:G.NT * 256].rearrange("p (n f) -> p n f", f=256)
    G.x = [M.dram(f"x{j}", [G.ROWS, 256]) for j in range(4)]
    s_x, s_xs = M.sem("s_x"), M.sem("s_xs")
    with nc.Block() as block:

        @block.gpsimd
        def _(pool):
            for n in range(G.NT):
                pool.indirect_dma_start(out=G.x_all[:, n, :], out_offset=None, in_=x, in_offset=bass.IndirectOffsetOnAxis(
                    ap=G.ids_in[:, n:n + 1], axis=0)).then_inc(s_x, 16)

        @block.sync
        def _(sp):
            sp.wait_ge(s_x, 16 * G.NT)
            sp.dma_start(G.x[0][0:G.PAD_ROW].rearrange("(n p) f -> p n f", p=P), G.x_all).then_inc(s_xs, 16)
            sp.wait_ge(s_xs, 16)


class Layer:

    def __init__(self, name, kind, lst, heads, width, row, table=None, own_from=None, x_in=None, x_out=None,
                 self_loop=True, norm=False, norm_of=None, sum_weights=False, scale_out=False, stores=(),
                 weight=None, bias_row=None, depth=0, out_width=0, finish=None, out=None):
        self.name, self.kind, self.list = name, kind, lst
        self.heads, self.width = heads, width
        self.row, self.own_width = row, row
        self.table, self.own_from = table, own_from
        self.x_in, self.x_out = x_in, x_out
        self.self_loop = self_loop
        self.norm, self.norm_of = norm, norm_of
        self.sum_weights = sum_weights
        self.scale_out = scale_out
        self.stores = stores
        self.weight, self.bias_row, self.depth, self.out_width = weight, bias_row, depth, out_width
        self.finish = finish or finish_none
        self.out = out


def layer(nc, M, G, L):
    NT = G.NT
    kind, k = L.kind, L.list
    H, F, R = L.heads, L.width, L.row
    HD = F // H
    gat, gcn, mx, pre = kind == "gat", kind == "gcn", kind == "max", kind == "pre"
    name = L.name
    sem = lambda x: M.sem(f"{name}_{x}")
    S = Named()
    S.logits, S.probs, S.diag, S.group, S.corr = sem("logits"), sem("probs"), sem("diag"), sem("group"), sem("corr")
    S.sums, S.evac, S.acc = sem("sums"), sem("evac"), sem("acc")
    S.z, S.var, S.dev, S.turned, S.zt = sem("z"), sem("var"), sem("dev"), sem("turned"), sem("zt")
    S.wide, S.row, S.stored = sem("wide"), sem("row"), sem("stored")
    S.mark, S.out = sem("mark"), sem("out")
    listed, rows, free, own_in, x_here, st = ([sem(f"{x}{b}") for b in range(2)] for x in
                                              ("listed", "rows", "free", "own", "x", "st"))
    sums = G.banks[0]
    turned = G.banks[1]
    wide = [G.banks[2], G.banks[3]]
    per_gather = GROUP if mx else 2
    if not pre:
        gbuf = G.store[:, 0:2 * SLOTS * R].rearrange("p (b s r) -> p b s r", b=2, s=SLOTS)
        lst = [G.lst[:, b, :, :] for b in range(2)]
        own = [G.own[:, b, 0:L.own_width] for b in range(2)]
        diag = [G.work[:, j * 16 * P:j * 16 * P + H * GROUP * P].rearrange("p (h s m) -> p h s m", h=H, m=P)
                for j in range(2)]
        corr = G.corr[:, 0:H * P].rearrange("p (h m) -> p h m", m=P)
        logits = G.logits[:, 0:H, :]
        probs = G.probs[:, 0:H, :]
        lists = G.lists[k].rearrange("(q p s) c -> q p (s c)", p=P, s=SLOTS)
    KT, WD = L.depth, L.out_width
    has_store_x = L.x_out is not None
    count = len(L.stores) + has_store_x
    own_late = mx or not L.self_loop

    class Counts:

        def __init__(self, eng):
            self.eng = eng
            self.tmp = eng.alloc_register(f"{name}_tmp")
            self.before = eng.alloc_register(f"{name}_before")
            eng.reg_mov(self.before, 0)

        def add(self, reg, v):
            self.eng.reg_alu(reg, reg, v, ALU.add)

        def wait(self, semaphore, reg, v):
            self.eng.reg_mov(self.tmp, v)
            self.eng.reg_alu(self.tmp, self.tmp, reg, ALU.add)
            self.eng.wait_ge(semaphore, self.tmp)

    def bounds(eng, n, only=None):
        v = [eng.value_load(G.bounds[k][0:1, bass.ds(n * HEADER + j, 1)], min_val=lo, max_val=hi)
             for j, lo, hi in ((0, 1, G.E), (1, 1, G.MAX_ITEMS), (2, 0, G.MAX_ITEMS), (3, 0, G.MAX_ITEMS),
                               (4, 0, G.E)) if only is None or j == only]
        return v if only is None else v[0]

    landed_reg = {}

    def gathered(eng, n):
        if eng.engine not in landed_reg:
            landed_reg[eng.engine] = eng.alloc_register(f"{name}_landed")
        return [eng.value_load(G.bounds[k][0:1, bass.ds((n + m) * HEADER + (7 if mx else 6), 1)], min_val=lo,
                               max_val=2 * G.E + 4 * NT) for m, lo in ((0, 0), (2, 1))] + [landed_reg[eng.engine]]

    def rows_landed(eng, b, so_far, c):
        full = so_far[0] + c * SLOTS + SLOTS
        eng.reg_mov(so_far[2], full)
        eng.reg_alu(so_far[2], so_far[2], so_far[1], ALU.min)
        eng.reg_alu(so_far[2], so_far[2], 16, ALU.mult)
        eng.wait_ge(rows[b], so_far[2])

    def walk(eng, agg, post):
        pairs = (NT - 1) // 2
        assert NT == 2 * pairs + 1
        if pre:
            with eng.Fori(0, pairs) as i:
                post(i * 2, 0, i, None)
                post(i * 2 + 1, 1, i, None)
            post(NT - 1, 0, pairs, None)
            return
        agg(0, 0, 0)
        with eng.Fori(0, pairs) as i:
            done = agg(i * 2 + 1, 1, i)
            post(i * 2, 0, i, done)
            done = agg(i * 2 + 2, 0, i + 1)
            post(i * 2 + 1, 1, i, done)
        done = None
        if post is not None:
            last = eng.value_load(G.bounds[k][0:1, NT * HEADER + 2:NT * HEADER + 3], min_val=NT, max_val=G.MAX_ITEMS)
            post(NT - 1, 0, pairs, last)

    with nc.Block() as block:

        @block.gpsimd
        def _(pool):
            if pre:
                return

            def agg(n, b, t):
                K, chunks, before, same, _ = bounds(pool, n)
                with pool.Fori(0, chunks) as c:
                    pool.wait_ge(listed[b], (same + c) * 16 + 16)
                    pool.sem_inc(S.mark, 1)
                    for j in range(0, SLOTS, per_gather):
                        with pool.If(K - c * SLOTS > j):
                            for s in range(j, j + per_gather):
                                pool.indirect_dma_start(
                                    out=gbuf[:, b, s, :], out_offset=None, in_=L.table[0:G.PAD_ROW + 1, :],
                                    in_offset=bass.IndirectOffsetOnAxis(ap=lst[b][:, s, 0:1], axis=0)
                                ).then_inc(rows[b], 16)

            def scatter(n, b):
                pool.wait_ge(S.z, n + 1)
                pool.sem_inc(S.mark, 1)
                pool.indirect_dma_start(out=L.out, out_offset=bass.IndirectOffsetOnAxis(ap=G.ids_t[:, b:b + 1], axis=0),
                                        in_=G.xn[:, b, :], in_offset=None, bounds_check=last_node,
                                        oob_is_err=False).then_inc(S.out, 16)

            def scattered(n):
                pool.wait_ge(S.out, n * 16 + 16)
                pool.sem_inc(S.stored, 1)

            if not mx:
                agg(0, 0, 0)
                with pool.Fori(0, (NT - 1) // 2) as i:
                    agg(i * 2 + 1, 1, i)
                    agg(i * 2 + 2, 0, i)
            else:
                last_node = pool.to_reg(G.N - 1)
                pool.sem_inc(S.stored, 2)
                agg(0, 0, 0)
                agg(1, 1, 0)
                agg(2, 0, 0)
                scatter(0, 0)
                with pool.Fori(0, (NT - 3) // 2) as i:
                    agg(i * 2 + 3, 1, i)
                    scattered(i * 2)
                    scatter(i * 2 + 1, 1)
                    agg(i * 2 + 4, 0, i)
                    scattered(i * 2 + 1)
                    scatter(i * 2 + 2, 0)
                for n in (NT - 2, NT - 1):
                    scattered(n - 1)
                    scatter(n, n % 2)
                scattered(NT - 1)

        @block.sync
        def _(sp):
            if pre:
                return

            def agg(n, b, t):
                K, chunks, before, same, _ = bounds(sp, n)
                with sp.Fori(0, chunks) as c:
                    sp.wait_ge(free[b], same + c + 1)
                    sp.dma_start(lst[b].rearrange("p s c -> p (s c)"),
                                 lists[bass.ds(before + c, 1)].rearrange("q p s -> (q p) s")).then_inc(listed[b], 16)

            agg(0, 0, 0)
            with sp.Fori(0, (NT - 1) // 2) as i:
                agg(i * 2 + 1, 1, i)
                agg(i * 2 + 2, 0, i)

        @block.scalar
        def _(act):
            counts = Counts(act)

            def load_own(n, b):
                act.dma_start(own[b], L.own_from[bass.ds(n * P, P), :]).then_inc(own_in[b], 16)

            def load_x(n, b):
                act.dma_start(G.xt[:, b, :], L.x_in[bass.ds(n * P, P), :]).then_inc(x_here[b], 16)

            def own_of_next(n, b, t):
                if own_late:
                    return
                if isinstance(n, int):
                    load_own(n + 2, b)
                else:
                    with act.If(t < (NT - 1) // 2 - b):
                        load_own(n + 2, b)

            def agg(n, b, t):
                chunks = bounds(act, n, 1)
                if L.self_loop and not mx:
                    act.wait_ge(own_in[b], (t + 1) * 16)
                    act.copy(G.acc[:, b, 0:F], own[b][:, 0:F]).then_inc(S.acc, 1)
                if mx:
                    return None
                with act.Fori(0, chunks) as c:
                    if gat:
                        counts.wait(S.logits, counts.before, c + 1)
                        act.activation(probs, logits, ACT.Exp).then_inc(S.probs, 1)
                    counts.wait(S.sums, counts.before, c + 2)
                    act.copy(G.acc[:, b, 0:F], sums[:, 0:F]).then_inc(S.evac, 1)
                    act.drain().then_inc(free[b], 1)
                counts.add(counts.before, chunks)
                own_of_next(n, b, t)

            def post(n, b, t, done):
                if L.norm:
                    act.wait_ge(S.var, n + 1)
                    act.activation(G.dev[:, :], G.mv[:, 1:2], ACT.Sqrt).then_inc(S.dev, 1)
                if not pre:
                    load_next(n, b, t)
                if mx:
                    return
                act.wait_ge(S.turned, n + 2)
                act.copy(G.zt[:, 0:KT * P], turned[:, 0:KT * P]).then_inc(S.zt, 1)
                if has_store_x:
                    act.dma_start(L.x_out[bass.ds(n * P, P), :], G.xn[:, b, :]).then_inc(st[b], 16)
                act.wait_ge(S.wide, n + 1)
                act.wait_ge(st[b], t * (16 * count) + 16 * count)
                scale = G.dinv[:, bass.ds(n, 1)] if L.scale_out else 1.0
                if L.scale_out:
                    act.activation(G.row[:, b, 0:min(WD, 512)], wide[0][:, 0:min(WD, 512)], ACT.Copy, scale=scale)
                else:
                    act.copy(G.row[:, b, 0:min(WD, 512)], wide[0][:, 0:min(WD, 512)])
                if WD > 512:
                    act.copy(G.row[:, b, 512:WD], wide[1][:, 0:WD - 512])
                act.drain().then_inc(S.row, 1)
                act.wait_ge(S.row, n + 2)
                for to, lo, hi in L.stores:
                    act.dma_start(to[bass.ds(n * P, P), :], G.row[:, b, lo:hi]).then_inc(st[b], 16)

            def load_next(n, b, t):
                if not (own_late or L.x_in is not None) or isinstance(n, int):
                    return

                def load():
                    act.wait_ge(S.z, n + 1)
                    if own_late:
                        load_own(n + 2, b)
                    if L.x_in is not None:
                        load_x(n + 2, b)

                if b == 0:
                    load()
                else:
                    with act.If(t < (NT - 1) // 2 - 1):
                        load()

            if not pre:
                for b in range(2):
                    load_own(b, b)
                    if L.x_in is not None:
                        load_x(b, b)
                act.sem_inc(S.evac, 1)
                for b in range(2):
                    act.sem_inc(free[b], 1)
            act.sem_inc(S.zt, 1)
            act.sem_inc(S.row, 1)
            if not mx:
                for b in range(2):
                    act.sem_inc(st[b], 16 * count)
            walk(act, agg, post)
            if not mx:
                for b in range(2):
                    act.wait_ge(st[b], ((NT + 1 - b) // 2 + 1) * 16 * count)

        @block.tensor
        def _(pe):
            def agg(n, b, t):
                if mx:
                    return
                K, chunks, before, same, groups = bounds(pe, n)
                so_far = gathered(pe, n) if gcn else None
                with pe.Fori(0, chunks) as c:
                    if gcn:
                        rows_landed(pe, b, so_far, c)
                    pe.wait_ge(S.evac, before + c + 1)
                    for g in range(NGROUP):
                        with pe.If(K - c * SLOTS > g * GROUP):
                            pe.wait_ge(S.diag, groups + c * NGROUP + (g + 1))
                            for s in range(GROUP):
                                for h in range(H):
                                    mm = pe.matmul(sums[:, h * HD:(h + 1) * HD], lhsT=diag[g % 2][:, h, s, :],
                                                   rhs=gbuf[:, b, g * GROUP + s, h * HD:(h + 1) * HD],
                                                   start=(g == 0 and s == 0 and h == 0), stop=True,
                                                   skip_group_check=True)
                            mm.then_inc(S.group, 1)
                    pe.wait_ge(S.acc, n + 1)
                    if gat:
                        pe.wait_ge(S.corr, before + c + 1)
                    for h in range(H):
                        mm = pe.matmul(sums[:, h * HD:(h + 1) * HD], lhsT=corr[:, h, :] if gat else G.ident[:, :],
                                       rhs=G.acc[:, b, h * HD:(h + 1) * HD], start=False, stop=True,
                                       skip_group_check=True)
                    mm.then_inc(S.sums, 1)

            def post(n, b, t, done):
                if mx:
                    return
                pe.wait_ge(S.z, n + 1)
                pe.wait_ge(S.zt, n + 1)
                for j in range(KT):
                    mm = pe.transpose(turned[:, j * P:(j + 1) * P], G.z[:, j * P:(j + 1) * P], G.ident[:, :])
                mm.then_inc(S.turned, 1)
                pe.wait_ge(S.zt, n + 2)
                pe.wait_ge(S.row, n + 1)
                for lo in range(0, WD, 512):
                    hi = min(WD, lo + 512)
                    out = wide[lo // 512][:, 0:hi - lo]
                    for j in range(KT):
                        mm = pe.matmul(out, lhsT=G.zt[:, j * P:(j + 1) * P], rhs=L.weight[:, j, lo:hi],
                                       start=(j == 0), stop=(j == KT - 1 and L.bias_row is None))
                    if L.bias_row is not None:
                        mm = pe.matmul(out, lhsT=G.one_row[:, :], rhs=L.bias_row[:, lo:hi], start=False, stop=True)
                mm.then_inc(S.wide, 1)

            if not pre:
                pe.sem_inc(S.group, 2)
                pe.sem_inc(S.sums, 1)
            pe.sem_inc(S.turned, 1)
            walk(pe, agg, post)

        @block.vector
        def _(dve):
            def agg(n, b, t):
                K, chunks, before, same, groups = bounds(dve, n)
                so_far = gathered(dve, n) if gat or mx else None
                gb = gbuf[:, b, :, :]
                m, den = G.m[:, b, 0:H], G.den[:, b, 0:H]
                if not gcn:
                    dve.wait_ge(own_in[b], (t + 1) * 16)
                if gat:
                    if L.self_loop:
                        dve.tensor_tensor(m, own[b][:, F:F + H], own[b][:, F + H:F + 2 * H], ALU.add)
                        dve.drain()
                        dve.scalar_tensor_tensor(out=m, in0=m, scalar=SLOPE, in1=m, op0=ALU.mult, op1=ALU.max)
                        dve.memset(den, 1.0)
                    else:
                        dve.memset(m, NEG)
                        dve.memset(den, 0.0)
                        dve.memset(G.acc[:, b, 0:F], 0.0).then_inc(S.acc, 1)
                elif mx:
                    dve.memset(G.acc[:, b, 0:F], LOWEST)
                if L.sum_weights:
                    dve.memset(G.wsum[:, :], 1.0)
                if not gcn:
                    dve.drain()
                with dve.Fori(0, chunks) as c:
                    dve.wait_ge(listed[b], (same + c) * 16 + 16)
                    if L.sum_weights:
                        dve.tensor_reduce(G.wpart[:, :], lst[b][:, :, 1].bitcast(F32), AX.X, ALU.add)
                    if gat:
                        dve.tensor_scalar(G.mask[:, :], lst[b][:, :, 0], float(G.PAD_ROW), NEG, ALU.is_equal, ALU.mult)
                    if gat or mx:
                        rows_landed(dve, b, so_far, c)
                    if gat:
                        lg = logits[:, :, 0:SLOTS]
                        dve.tensor_tensor(lg, gb[:, :, F:F + H].rearrange("p s h -> p h s"),
                                          bc(own[b][:, F + H:F + 2 * H], 2, SLOTS), ALU.add)
                        dve.drain()
                        if L.sum_weights:
                            dve.tensor_tensor(G.wsum[:, :], G.wsum[:, :], G.wpart[:, :], ALU.add)
                        dve.scalar_tensor_tensor(out=lg, in0=lg, scalar=SLOPE, in1=lg, op0=ALU.mult, op1=ALU.max)
                        dve.drain()
                        dve.tensor_tensor(lg, lg, bc(G.mask[:, :], 1, H), ALU.add)
                        dve.drain()
                        dve.tensor_reduce(G.mnew[:, 0:H], lg, AX.X, ALU.max)
                        dve.drain()
                        dve.tensor_tensor(G.mnew[:, 0:H], G.mnew[:, 0:H], m, ALU.max)
                        dve.drain()
                        dve.tensor_tensor(lg, lg, bc(G.mnew[:, 0:H], 2, SLOTS), ALU.subtract)
                        dve.tensor_tensor(logits[:, :, SLOTS], m, G.mnew[:, 0:H], ALU.subtract)
                        dve.drain().then_inc(S.logits, 1)
                        dve.tensor_copy(m, G.mnew[:, 0:H])
                        dve.wait_ge(S.probs, before + c + 1)
                        dve.tensor_tensor(den, den, probs[:, :, SLOTS], ALU.mult)
                        dve.tensor_reduce(G.dsum[:, 0:H], probs[:, :, 0:SLOTS], AX.X, ALU.add)
                        dve.drain()
                        dve.tensor_tensor(den, den, G.dsum[:, 0:H], ALU.add)
                    if gat or gcn:
                        for g in range(NGROUP):
                            with dve.If(K - c * SLOTS > g * GROUP):
                                dve.wait_ge(S.group, groups + c * NGROUP + (g + 1 + (g == 0)))
                                if gat:
                                    wts = probs[:, :, g * GROUP:(g + 1) * GROUP]
                                else:
                                    wts = lst[b][:, g * GROUP:(g + 1) * GROUP, 1].bitcast(F32).unsqueeze(1)
                                dve.tensor_tensor(diag[g % 2].rearrange("p h s m -> p (h s) m"),
                                                  bc(G.ident[:, :], 1, H * GROUP),
                                                  bc(wts, 3, P).rearrange("p h s m -> p (h s) m") if H == 1 else
                                                  bc(wts, 3, P), ALU.mult).then_inc(S.diag, 1)
                        if gat:
                            dve.wait_ge(S.sums, before + c + 1)
                            dve.tensor_tensor(corr, bc(G.ident[:, :], 1, H), bc(probs[:, :, SLOTS], 2, P),
                                              ALU.mult).then_inc(S.corr, 1)
                    if mx:
                        for g in range(NGROUP):
                            with dve.If(K - c * SLOTS > g * GROUP):
                                dve.tensor_reduce(G.part[:, g, :], gb[:, g * GROUP:(g + 1) * GROUP, :].rearrange(
                                    "p s f -> p f s"), AX.X, ALU.max)
                            with dve.Else():
                                dve.memset(G.part[:, g, :], LOWEST)
                        dve.drain().then_inc(free[b], 1)
                        dve.tensor_reduce(G.z[:, 0:F], G.part.rearrange("p g f -> p f g"), AX.X, ALU.max)
                        dve.drain()
                        dve.tensor_tensor(G.acc[:, b, 0:F], G.acc[:, b, 0:F], G.z[:, 0:F], ALU.max)
                        dve.drain()
                if L.sum_weights:
                    dve.drain()
                    dve.tensor_copy(G.wdeg[:, bass.ds(n, 1)], G.wsum[:, :])
                return before

            def post(n, b, t, done):
                acc, xn, xt, z = G.acc[:, b, :], G.xn[:, b, :], G.xt[:, b, :], G.z
                if not pre:
                    if not mx:
                        dve.wait_ge(S.evac, done + 1)
                    if gat:
                        dve.reciprocal(G.rden[:, 0:H], G.den[:, b, 0:H])
                        if not L.self_loop:
                            dve.tensor_scalar(G.some[:, 0:H], G.m[:, b, 0:H], NEG * 0.1, None, ALU.is_gt)
                            dve.tensor_scalar(G.none[:, 0:H], G.m[:, b, 0:H], NEG * 0.1, None, ALU.is_le)
                        dve.drain()
                        if not L.self_loop:
                            dve.tensor_tensor(G.rden[:, 0:H], G.rden[:, 0:H], G.some[:, 0:H], ALU.mult)
                            dve.drain()
                if L.x_in is not None:
                    dve.wait_ge(x_here[b], t * 16 + 16)
                if has_store_x:
                    dve.wait_ge(st[b], t * (16 * count) + 16 * count)
                elif mx:
                    dve.wait_ge(S.stored, n + 1)
                if mx:
                    dve.tensor_copy(G.ids_t[:, b:b + 1], G.ids_i[:, bass.ds(n, 1)])
                else:
                    dve.wait_ge(S.turned, n + 1)
                L.finish(dve, G, n, b, acc, xn, xt, z, own[b] if not pre else None)
                if L.norm:
                    source = L.norm_of(G, n, b)
                    if not pre:
                        dve.drain()
                    dve.bn_stats(G.stats[:, :], source)
                    dve.drain()
                    dve.bn_aggr(G.mv[:, :], G.stats[:, :])
                    dve.drain()
                    dve.tensor_scalar(G.mv[:, 1:2], G.mv[:, 1:2], LN_EPS, None, ALU.add)
                    dve.drain().then_inc(S.var, 1)
                    dve.wait_ge(S.dev, n + 1)
                    dve.reciprocal(G.dev2[:, :], G.dev[:, :])
                    dve.drain()
                    dve.tensor_scalar(z[:, 0:256], source, G.mv[:, 0:1], G.dev2[:, :], ALU.subtract, ALU.mult)
                    dve.drain()
                    dve.tensor_scalar(z[:, 0:256], z[:, 0:256], 0.0, None, ALU.max)
                dve.drain().then_inc(S.z, 1)

            walk(dve, agg, post)

    M.end_phase()


def finish_none(dve, G, n, b, acc, xn, xt, z, own):
    pass


def finish_gat1(dve, G, n, b, acc, xn, xt, z, own):
    for h in range(4):
        c = slice(h * P, (h + 1) * P)
        dve.scalar_tensor_tensor(out=z[:, c], in0=acc[:, c], scalar=G.rden[:, h:h + 1], in1=G.b1[:, c],
                                 op0=ALU.mult, op1=ALU.add)
    dve.drain()
    dve.tensor_scalar(G.neg[:, :], z[:, 0:512], 0.0, G.slope[:, 0:1], ALU.min, ALU.mult)
    dve.drain()
    dve.scalar_tensor_tensor(out=z[:, 0:512], in0=z[:, 0:512], scalar=0.0, in1=G.neg[:, :], op0=ALU.max, op1=ALU.add)


def finish_gat2(dve, G, n, b, acc, xn, xt, z, own):
    dve.scalar_tensor_tensor(out=xn, in0=acc[:, 0:256], scalar=G.rden[:, 0:1], in1=G.b2[:, :],
                             op0=ALU.mult, op1=ALU.add)
    dve.drain()
    dve.tensor_tensor(xn, xn, xt, ALU.add)


def finish_gat3(dve, G, n, b, acc, xn, xt, z, own):
    for h in range(2):
        c = slice(h * P, (h + 1) * P)
        dve.scalar_tensor_tensor(out=xn[:, c], in0=acc[:, c], scalar=G.rden[:, h:h + 1], in1=xt[:, c],
                                 op0=ALU.mult, op1=ALU.add)
    dve.drain()
    for h in range(2):
        c = slice(h * P, (h + 1) * P)
        dve.scalar_tensor_tensor(out=xn[:, c], in0=own[:, c], scalar=G.none[:, h:h + 1], in1=xn[:, c],
                                 op0=ALU.mult, op1=ALU.add)


def finish_gcn1(dve, G, n, b, acc, xn, xt, z, own):
    dve.scalar_tensor_tensor(out=z[:, 0:256], in0=acc[:, 0:256], scalar=G.dinv[:, bass.ds(n, 1)], in1=G.b4[:, :],
                             op0=ALU.mult, op1=ALU.add)
    dve.drain()
    dve.tensor_scalar(z[:, 0:256], z[:, 0:256], 0.0, None, ALU.max)


def finish_gcn2(dve, G, n, b, acc, xn, xt, z, own):
    dve.scalar_tensor_tensor(out=xn, in0=acc[:, 0:256], scalar=G.dinv[:, bass.ds(n, 1)], in1=G.b5[:, :],
                             op0=ALU.mult, op1=ALU.add)
    dve.drain()
    dve.scalar_tensor_tensor(out=xn, in0=xn, scalar=0.0, in1=xt, op0=ALU.max, op1=ALU.add)


def finish_max(dve, G, n, b, acc, xn, xt, z, own):
    dve.tensor_tensor(xn, own, acc[:, 0:256], ALU.add)
    dve.drain()
    dve.scalar_tensor_tensor(out=xn, in0=xn, scalar=0.0, in1=xt, op0=ALU.max, op1=ALU.add)


def inverse_degrees(nc, M, G):
    s1, s2 = M.sem("s_deg"), M.sem("s_root")
    with nc.Block() as block:

        @block.vector
        def _(dve):
            dve.tensor_scalar(G.wroot[:, :], G.wdeg[:, :], 1.2e-35, None, ALU.max)
            dve.drain().then_inc(s1, 1)
            dve.tensor_scalar(G.wdeg[:, :], G.wdeg[:, :], 0.0, None, ALU.is_gt)
            dve.wait_ge(s2, 1)
            dve.reciprocal(G.dinv[:, :], G.dinv[:, :])
            dve.drain()
            dve.tensor_tensor(G.dinv[:, :], G.dinv[:, :], G.wdeg[:, :], ALU.mult)

        @block.scalar
        def _(act):
            act.wait_ge(s1, 1)
            act.activation(G.dinv[:, :], G.wroot[:, :], ACT.Sqrt).then_inc(s2, 1)


def clear_rows(nc, M, G):
    half = G.store.shape[1] // 2
    with nc.Block() as block:

        @block.vector
        def _(dve):
            dve.memset(G.store[:, 0:half], 0.0)

        @block.gpsimd
        def _(pool):
            pool.memset(G.store[:, half:], 0.0)


def graph_network(nc, a, out):
    with ExitStack() as ctx:
        M = Mem(nc, ctx)
        G = kernel_shapes(a.x.shape[0], a.src.shape[0])
        NT = G.NT
        G.banks = [M.ps(f"bank{j}", [P, 512]) for j in range(8)]
        G.store = M.sb("store", [P, 2 * SLOTS * 520])
        G.work = M.sb("work", [P, 2 * 16 * P])
        top = [0]

        def arena(name, n, dt=F32):
            at, top[0] = top[0], top[0] + n
            assert top[0] <= G.store.shape[1], (name, top[0])
            return G.store[:, at:at + n] if dt is F32 else G.store[:, at:at + n].bitcast(dt)

        G.early = M.sb("early", [P, TILES_AT_ONCE * P])

        constants(nc, M, G)
        G.before = [arena(f"before{k}", G.ET * NT) for k in (IN, OUT)]
        keep = top[0]
        edge_keys(nc, M, G, arena, a.src, a.dst, a.edge_weight)
        top[0] -= 4 * 4 * P
        histograms(nc, M, G, arena)
        top[0] = keep
        node_order(nc, M, G, arena)
        top[0] = keep
        scatter_edges(nc, M, G, arena)
        M.end_phase()
        G.arena_at = NT * 256
        weights(nc, M, G, a)

        G.corr = M.sb("corr", [P, 4 * P])
        G.lst = M.sb("lst", [P, 2, SLOTS, 2], I32)
        G.own = M.sb("own", [P, 2, 520])
        G.acc = M.sb("acc", [P, 2, 512])
        G.xt = M.sb("xt", [P, 2, 256])
        G.xn = M.sb("xn", [P, 2, 256])
        G.z = M.sb("z", [P, 512])
        G.zt = M.sb("zt", [P, 512])
        G.row = M.sb("row", [P, 2, 520])
        G.neg = G.xn[:, :, :].rearrange("p b f -> p (b f)")
        G.logits = M.sb("logits", [P, 4, SLOTS + 1])
        G.probs = M.sb("probs", [P, 4, SLOTS + 1])
        G.mask = M.sb("mask", [P, SLOTS])
        G.mnew = M.sb("mnew", [P, 4])
        G.dsum = M.sb("dsum", [P, 4])
        G.rden = M.sb("rden", [P, 4])
        G.some = M.sb("some", [P, 4])
        G.none = M.sb("none", [P, 4])
        G.stats = M.sb("stats", [P, 6])
        G.mv = M.sb("mv", [P, 2])
        G.dev = M.sb("dev", [P, 1])
        G.dev2 = M.sb("dev2", [P, 1])
        G.wsum = M.sb("wsum", [P, 1])
        G.wpart = M.sb("wpart", [P, 1])
        G.wdeg = M.sb("wdeg", [P, NT])
        G.wroot = M.sb("wroot", [P, NT])
        G.dinv = M.sb("dinv", [P, NT])
        G.m = M.sb("m", [P, 2, 4])
        G.den = M.sb("den", [P, 2, 4])
        G.ids_t = M.sb("ids_t", [P, 2], I32)
        G.part = G.work[:, 0:NGROUP * 256].rearrange("p (g f) -> p g f", f=256)

        first_rows(nc, M, G, a.x)
        T = G.tables

        def of_x(G, n, b):
            return G.x_all[:, bass.ds(n, 1), :].rearrange("p o f -> p (o f)")

        def of_xn(G, n, b):
            return G.xn[:, b, :]

        layer(nc, M, G, Layer("pre", "pre", IN, 1, 256, 0, norm=True, norm_of=of_x, stores=[(T[0][0:G.PAD_ROW], 0, 520)],
                          weight=G.W1, depth=2, out_width=520))
        clear_rows(nc, M, G)
        layer(nc, M, G, Layer("gat1", "gat", IN, 4, 512, 520, table=T[0], own_from=T[0], sum_weights=True,
                          stores=[(T[1][0:G.PAD_ROW], 0, 258)], weight=G.W2, depth=4, out_width=258, finish=finish_gat1))
        inverse_degrees(nc, M, G)
        layer(nc, M, G, Layer("gat2", "gat", IN, 1, 256, 258, table=T[1], own_from=T[1], x_in=G.x[0], x_out=G.x[1],
                          norm=True, norm_of=of_xn, stores=[(T[2][0:G.PAD_ROW], 0, 260)], weight=G.W3,
                          bias_row=G.row3, depth=2, out_width=260, finish=finish_gat2))
        layer(nc, M, G, Layer("gat3", "gat", OUT, 2, 256, 260, table=T[2], own_from=T[2], x_in=G.x[1], x_out=G.x[2],
                          self_loop=False, norm=True, norm_of=of_xn, scale_out=True,
                          stores=[(T[3][0:G.PAD_ROW], 0, 256)], weight=G.W4, depth=2, out_width=256, finish=finish_gat3))
        layer(nc, M, G, Layer("gcn1", "gcn", IN, 1, 256, 256, table=T[3], own_from=T[3], scale_out=True,
                          stores=[(T[4][0:G.PAD_ROW], 0, 256)], weight=G.W5, depth=2, out_width=256, finish=finish_gcn1))
        layer(nc, M, G, Layer("gcn2", "gcn", IN, 1, 256, 256, table=T[4], own_from=T[4], x_in=G.x[2], x_out=G.x[3],
                          norm=True, norm_of=of_xn, stores=[(T[5][0:G.PAD_ROW], 0, 256), (G.own6, 256, 512)],
                          weight=G.W6, bias_row=G.row6, depth=2, out_width=512, finish=finish_gcn2))
        layer(nc, M, G, Layer("edge", "max", IN, 1, 256, 256, table=T[5], own_from=G.own6, x_in=G.x[3],
                          finish=finish_max, out=out))


def kernel(**inputs):
    import concourse.bacc as bacc
    from concourse.bass_utils import run_bass_kernel_spmd as run

    nc = bacc.Bacc("TRN2", target_bir_lowering=False, num_devices=1)
    arrays, aps = {}, {}
    for name, v in inputs.items():
        v = np.ascontiguousarray(v)
        if v.ndim == 0:
            v = v.reshape(1, 1)
        arrays[f"in_{name}"] = v
        aps[name] = nc.dram_tensor(f"in_{name}", v.shape, mybir.dt.from_np(v.dtype), kind="ExternalInput").ap()
    N, D = inputs["x"].shape
    out = nc.dram_tensor("out", (N, D), F32, kind="ExternalOutput").ap()
    a = Named()
    a.x = aps["x"]
    a.src = aps["src"]
    a.dst = aps["dst"]
    a.edge_weight = aps["edge_weight"]
    a.W1 = aps["L0_gnn_W1"]
    a.as1 = aps["L0_gnn_a_src1"]
    a.ad1 = aps["L0_gnn_a_dst1"]
    a.b1 = aps["L0_gnn_b1"]
    a.slope = aps["L0_gnn_prelu_w"]
    a.W2 = aps["L0_gnn_W2"]
    a.as2 = aps["L0_gnn_a_src2"]
    a.ad2 = aps["L0_gnn_a_dst2"]
    a.b2 = aps["L0_gnn_b2"]
    a.W3 = aps["L1_gnn_W_w"]
    a.b3 = aps["L1_gnn_W_b"]
    a.a3 = aps["L1_gnn_a"]
    a.W4 = aps["L2_gnn_W1"]
    a.b4 = aps["L2_gnn_b1"]
    a.W5 = aps["L2_gnn_W2"]
    a.b5 = aps["L2_gnn_b2"]
    a.theta = aps["L3_gnn_theta_w"]
    a.theta_b = aps["L3_gnn_theta_b"]
    a.phi = aps["L3_gnn_phi_w"]
    a.phi_b = aps["L3_gnn_phi_b"]
    graph_network(nc, a, out)
    r = run(nc, [arrays], core_ids=[0])
    return r.results[0]["out"]
```

```python
from contextlib import ExitStack

import numpy as np
import concourse.bass as bass
from concourse import mybir

P = 128
ALU = mybir.AluOpType
ACT = mybir.ActivationFunctionType
AX = mybir.AxisListType
F32 = mybir.dt.float32
I32 = mybir.dt.int32
BF16 = mybir.dt.bfloat16

SHIFT = 5
SLOTS = 1 << SHIFT
GROUP = 4
NGROUP = SLOTS // GROUP
KEYS = 64
TILES_AT_ONCE = 17
BIG = float(1 << 23)
NEG = -1.0e30
LOWEST = -3.0e38
LN_EPS = 1e-5
SLOPE = 0.2
IN, OUT = 0, 1
HEADER = 4


class Named:
    pass


def kernel_shapes(N, E):
    s = Named()
    s.N, s.E = N, E
    s.NT = -(-N // P)
    s.ET = -(-E // P)
    s.PAD_ROW = s.NT * P
    s.ROWS = s.PAD_ROW + 2 * P
    s.MAX_ITEMS = -(-E // SLOTS) + s.NT
    return s


class Mem:

    def __init__(self, nc, ctx):
        self.nc, self.ctx = nc, ctx
        self.phase_sems = []

    def sb(self, name, shape, dt=F32):
        return self.ctx.enter_context(self.nc.sbuf_tensor(name, shape, dt))

    def ps(self, name, shape):
        return self.ctx.enter_context(self.nc.psum_tensor(name, shape, F32))

    def dram(self, name, shape, dt=F32):
        return self.nc.dram_tensor(name, shape, dt, kind="Internal").ap()

    def sem(self, name):
        s = self.nc.alloc_semaphore(name=name)
        self.phase_sems.append(s)
        return s

    def end_phase(self):
        self.nc.all_engine_barrier()
        self.nc.clear_and_free_semaphores(self.phase_sems)
        self.nc.all_engine_barrier()
        self.phase_sems = []


def bc(ap, axis, n):
    u = ap.unsqueeze(axis)
    shape = list(u.shape)
    shape[axis] = n
    return u.broadcast_to(shape)


def constants(nc, M, G):
    G.ident = M.sb("ident", [P, P])
    G.ones_bf = M.sb("ones_bf", [P, P], BF16)
    G.lower_bf = M.sb("lower_bf", [P, P], BF16)
    G.lower = M.sb("lower", [P, P])
    G.upper = M.sb("upper", [P, P])
    G.same_parity = M.sb("same_parity", [32, 32])
    G.iota_row = M.sb("iota_row", [P, P])
    G.iota_col = M.sb("iota_col", [P, 1])
    G.ids = M.sb("ids", [P, G.NT])
    G.one_row = M.sb("one_row", [1, P])
    G.sc_i = M.sb("sc_i", [32, 32], I32)
    G.sc_i2 = M.sb("sc_i2", [32, 32], I32)
    G.s_const = M.sem("s_const")
    with nc.Block() as block:

        @block.gpsimd
        def _(pool):
            pool.memset(G.ident[:, :], 0.0)
            pool.memset(G.lower[:, :], 1.0)
            pool.memset(G.upper[:, :], 1.0)
            pool.memset(G.ones_bf[:, :], 1.0)
            pool.memset(G.one_row[:, :], 1.0)
            pool.drain()
            pool.affine_select(out=G.ident[:, :], in_=G.ident[:, :], compare_op=ALU.not_equal, fill=1.0,
                               base=0, pattern=[[-1, P]], channel_multiplier=1)
            pool.affine_select(out=G.lower[:, :], in_=G.lower[:, :], compare_op=ALU.is_gt, fill=0.0,
                               base=0, pattern=[[1, P]], channel_multiplier=-1)
            pool.affine_select(out=G.upper[:, :], in_=G.upper[:, :], compare_op=ALU.is_gt, fill=0.0,
                               base=0, pattern=[[-1, P]], channel_multiplier=1)
            pool.iota(G.iota_row[:, :], pattern=[[1, P]], base=0, channel_multiplier=0,
                      allow_small_or_imprecise_dtypes=True)
            pool.iota(G.iota_col[:, :], pattern=[[1, 1]], base=0, channel_multiplier=1,
                      allow_small_or_imprecise_dtypes=True)
            pool.iota(G.ids[:, :], pattern=[[P, G.NT]], base=0, channel_multiplier=1,
                      allow_small_or_imprecise_dtypes=True)
            pool.iota(G.sc_i[:, :], pattern=[[1, 32]], base=64, channel_multiplier=-1)
            pool.drain().then_inc(G.s_const, 1)

        @block.vector
        def _(dve):
            dve.wait_ge(G.s_const, 1)
            dve.tensor_copy(G.lower_bf[:, :], G.lower[:, :])
            dve.tensor_scalar(G.sc_i2[:, :], G.sc_i[:, :], 1, None, ALU.bitwise_and)
            dve.drain()
            dve.tensor_scalar(G.same_parity[:, :], G.sc_i2[:, :], 0.0, None, ALU.is_equal)
            dve.drain()
            dve.tensor_tensor(G.same_parity[:, :], G.same_parity[:, :], G.lower[0:32, 0:32], ALU.mult)


def edge_keys(nc, M, G, arena, src, dst, edge_weight):
    ET, E = G.ET, G.E
    full = E // ET
    rest = E - full * ET
    G.key_i = [arena(f"key_i{k}", ET, I32) for k in (IN, OUT)]
    G.lo_i = [arena(f"lo_i{k}", ET, I32) for k in (IN, OUT)]
    G.key = [G.work[:, k * ET:(k + 1) * ET] for k in (IN, OUT)]
    G.hi = [G.work[:, (2 + k) * ET:(3 + k) * ET] for k in (IN, OUT)]
    G.lo = [arena(f"lo{k}", ET) for k in (IN, OUT)]
    G.w = G.work[:, 4 * ET:5 * ET]
    G.rowT = arena("rowT", 4 * 4 * P)
    G.key_rows = M.dram("key_rows", [4, ET * P])
    s_pad, s_load, s_key, s_tr, s_cp, s_row = (M.sem(x) for x in
                                               ("s_pad", "s_load", "s_key", "s_tr", "s_cp", "s_row"))
    PT = G.banks
    nblk = -(-ET // P)
    with nc.Block() as block:

        @block.sync
        def _(sp):
            sp.wait_ge(s_pad, 1)
            for dst_t, a in ((G.key_i[IN], dst), (G.key_i[OUT], src), (G.w[:, :], edge_weight)):
                sp.dma_start(dst_t[0:full, :], a[0:full * ET].rearrange("(p t) -> p t", t=ET)).then_inc(s_load, 16)
                sp.dma_start(dst_t[full:full + 1, 0:rest],
                             a[full * ET:E].rearrange("(p t) -> p t", p=1)).then_inc(s_load, 16)
            sp.wait_ge(s_cp, 4)
            for q in range(4):
                for j in range(nblk):
                    m = min(P, ET - j * P)
                    sp.dma_start(G.key_rows[q, j * P * P:(j * P + m) * P].rearrange("(t p) -> t p", p=P),
                                 G.rowT[0:m, (q * 4 + j) * P:(q * 4 + j + 1) * P]).then_inc(s_row, 16)
            sp.wait_ge(s_row, 16 * 4 * nblk)

        @block.vector
        def _(dve):
            for k in (IN, OUT):
                dve.memset(G.key_i[k], G.PAD_ROW)
            dve.memset(G.w[:, :], 0.0)
            dve.drain().then_inc(s_pad, 1)
            dve.wait_ge(s_load, 96)
            for k in (IN, OUT):
                dve.tensor_scalar(G.lo_i[k], G.key_i[k], P - 1, None, ALU.bitwise_and)
                dve.tensor_copy(G.key[k][:, :], G.key_i[k])
            dve.drain()
            for k in (IN, OUT):
                dve.tensor_copy(G.lo[k], G.lo_i[k])
            dve.drain()
            for k in (IN, OUT):
                dve.tensor_tensor(G.hi[k][:, :], G.key[k][:, :], G.lo[k], ALU.subtract)
            dve.drain().then_inc(s_key, 1)
            for k in (IN, OUT):
                dve.tensor_scalar(G.hi[k][:, :], G.hi[k][:, :], 1.0 / P, None, ALU.mult)
            for q in range(4):
                dve.wait_ge(s_tr, q + 1)
                wide, m = (nblk - 1) * P, ET - (nblk - 1) * P
                dve.tensor_copy(G.rowT[:, q * 512:q * 512 + wide], PT[q][:, 0:wide])
                dve.tensor_copy(G.rowT[0:m, q * 512 + wide:(q + 1) * 512],
                                PT[q][0:m, wide:wide + P]).then_inc(s_cp, 1)

        @block.tensor
        def _(pe):
            pe.wait_ge(s_key, 1)
            for q, a in enumerate((G.key[IN][:, :], G.key[OUT][:, :], G.lo[IN], G.lo[OUT])):
                for j in range(nblk):
                    m = min(P, ET - j * P)
                    mm = pe.transpose(PT[q][0:m, j * P:(j + 1) * P], a[:, j * P:j * P + m], G.ident[:, :])
                mm.then_inc(s_tr, 1)


def histograms(nc, M, G, arena):
    TA, NT, ET = TILES_AT_ONCE, G.NT, G.ET
    steps = ET // TA
    assert steps * TA == ET and (TA + 1) * NT <= 512
    G.degree = [M.sb(f"degree{k}", [P, NT]) for k in (IN, OUT)]
    lo_hot = [arena(f"lo_hot{k}", TA * P // 2, BF16).rearrange("p (t b) -> p t b", t=TA) for k in (IN, OUT)]
    hi_hot = [arena(f"hi_hot{k}", TA * 26 // 2, BF16)[:, 0:TA * NT].rearrange("p (t a) -> p t a", t=TA)
              for k in (IN, OUT)]
    before = [b.rearrange("p (t a) -> p t a", a=NT) for b in G.before]
    s_hot, s_sum, s_read = ([M.sem(f"{x}{k}") for k in (IN, OUT)] for x in ("s_hot", "s_sum", "s_hread"))
    with nc.Block() as block:

        @block.vector
        def _(dve):
            for k in (IN, OUT):
                dve.memset(G.degree[k][:, :], 0.0)

            def hot(k, first):
                dve.tensor_tensor(lo_hot[k], bc(G.iota_row[:, :], 1, TA), bc(G.lo[k][:, bass.ds(first, TA)], 2, P),
                                  ALU.is_equal)
                dve.tensor_tensor(hi_hot[k], bc(G.iota_row[:, 0:NT], 1, TA), bc(G.hi[k][:, bass.ds(first, TA)], 2, NT),
                                  ALU.is_equal).then_inc(s_hot[k], 1)

            def read(k, i, first):
                dve.wait_ge(s_sum[k], i + 1)
                sums = G.banks[k][:, 0:(TA + 1) * NT].rearrange("p (t a) -> p t a", a=NT)
                at = before[k][:, bass.ds(first, TA), :]
                dve.tensor_copy(at[:, 0, :], G.degree[k][:, :])
                dve.tensor_tensor(at[:, 1:TA, :], sums[:, 1:TA, :], bc(G.degree[k][:, :], 1, TA - 1), ALU.add)
                dve.drain()
                dve.tensor_tensor(G.degree[k][:, :], G.degree[k][:, :], sums[:, TA, :], ALU.add).then_inc(s_read[k], 1)
                dve.drain()

            for k in (IN, OUT):
                hot(k, 0)
            dve.drain()
            with dve.Fori(0, steps - 1) as i:
                for k in (IN, OUT):
                    read(k, i, i * TA)
                    hot(k, i * TA + TA)
            for k in (IN, OUT):
                read(k, steps - 1, (steps - 1) * TA)

        @block.tensor
        def _(pe):
            with pe.Fori(0, steps) as i:
                for k in (IN, OUT):
                    pe.wait_ge(s_hot[k], i + 1)
                    pe.wait_ge(s_read[k], i + 1)
                    for j in range(TA):
                        mm = pe.matmul(G.banks[k][:, (j + 1) * NT:(TA + 1) * NT].rearrange("p (t a) -> p t a", a=NT),
                                       lhsT=lo_hot[k][:, j, :], rhs=bc(hi_hot[k][:, j, :], 1, TA - j),
                                       start=(j == 0), stop=(j == TA - 1), skip_group_check=True)
                    mm.then_inc(s_sum[k], 1)

        @block.sync
        def _(sp):
            for k in (IN, OUT):
                sp.sem_inc(s_read[k], 1)


def node_order(nc, M, G, arena):
    NT = G.NT
    AG = 5
    assert NT % AG == 0 and AG * KEYS <= 512
    cls = arena("cls", NT)
    hot = arena("cls_hot", NT * KEYS // 2, BF16).rearrange("p (a k) -> p a k", k=KEYS)
    cum = arena("cls_cum", (NT + 1) * KEYS // 2, BF16).rearrange("p (a k) -> p a k", k=KEYS)
    count = arena("cls_count", KEYS)
    suf = [arena(f"suf{j}", KEYS) for j in range(2)]
    rank = arena("rank", NT * KEYS).rearrange("p (a k) -> p a k", k=KEYS)
    G.base_pos = M.sb("base_pos", [P, 2, 2, NT])
    G.pos_i = M.sb("pos_i", [P, NT], I32)
    meta = arena("meta", NT * 4).rearrange("p (a q) -> p a q", q=4)
    G.meta = M.dram("meta", [G.PAD_ROW, 4])
    G.by_pos = M.sb("by_pos", [P, NT, 4])
    G.bounds_dram = M.dram("bounds_dram", [2, 32 * HEADER], I32)
    G.bounds = [M.sb(f"bounds{k}", [1, 32 * HEADER], I32) for k in (IN, OUT)]
    G.ids_i = M.sb("ids_i", [P, NT], I32)
    G.ids_in = M.sb("ids_in", [P, NT], I32)
    t_i = arena("t_i", 64, I32)
    t2_i = arena("t2_i", 64, I32)
    bnd = [arena(f"bnd{k}", HEADER) for k in (IN, OUT)]
    bnd_i = [arena(f"bnd_i{k}", HEADER, I32) for k in (IN, OUT)]
    kmax = arena("kmax", 2)
    tile_i = arena("tile_i", NT, I32)
    low_i = arena("low_i", NT, I32)
    tile_f = arena("tile_f", NT)
    low_f = arena("low_f", NT)
    tile_hot = arena("tile_hot", NT * NT).rearrange("p (a n) -> p a n", n=NT)
    picked = arena("picked", NT * NT).rearrange("p (a n) -> p a n", n=NT)
    first = [arena(f"first{k}", 32 * HEADER, I32) for k in (IN, OUT)]
    first_f = [arena(f"first_f{k}", NT) for k in (IN, OUT)]
    s_o = Named()
    s_o.hot = M.sem("s_o_hot")
    s_o.cum = M.sem("s_o_cum")
    s_o.count = M.sem("s_o_count")
    s_o.rank = M.sem("s_o_rank")
    s_o.read = M.sem("s_o_read")
    s_o.pos = M.sem("s_o_pos")
    s_o.meta = M.sem("s_o_meta")
    s_o.load = M.sem("s_o_load")
    s_o.tr = M.sem("s_o_tr")
    s_o.max = M.sem("s_o_max")
    s_o.cum2 = M.sem("s_o_cum2")
    s_o.bnd = M.sem("s_o_bnd")
    s_o.bst = M.sem("s_o_bst")
    s_o.bld = M.sem("s_o_bld")
    with nc.Block() as block:

        @block.vector
        def _(dve):
            dve.tensor_scalar(cls, G.degree[IN][:, :], float(KEYS - 1), None, ALU.min)
            dve.drain()
            dve.tensor_tensor(hot, bc(G.iota_row[:, 0:KEYS], 1, NT), bc(cls, 2, KEYS), ALU.is_equal)
            dve.memset(cum[:, 0, :], 0.0)
            dve.drain()
            for a in range(NT):
                dve.tensor_tensor(cum[:, a + 1, :], cum[:, a, :], hot[:, a, :], ALU.add)
                dve.drain()
            dve.drain().then_inc(s_o.hot, 1)
            dve.wait_ge(s_o.count, 1)
            dve.tensor_copy(count, G.banks[5][:, 0:KEYS])
            dve.drain()
            dve.tensor_copy(suf[0], count)
            dve.drain()
            cur, step = 0, 1
            while step < KEYS:
                dve.tensor_tensor(suf[1 - cur][:, 0:KEYS - step], suf[cur][:, 0:KEYS - step],
                                  suf[cur][:, step:KEYS], ALU.add)
                dve.tensor_copy(suf[1 - cur][:, KEYS - step:KEYS], suf[cur][:, KEYS - step:KEYS])
                dve.drain()
                cur, step = 1 - cur, 2 * step
            dve.tensor_tensor(count, suf[cur], count, ALU.subtract)
            dve.drain()
            dve.wait_ge(s_o.rank, NT // AG)
            for g in range(NT // AG):
                dve.tensor_tensor(rank[:, g * AG:(g + 1) * AG, :],
                                  G.banks[g][:, 0:AG * KEYS].rearrange("p (a k) -> p a k", k=KEYS),
                                  bc(count, 1, AG), ALU.add)
            dve.drain()
            dve.tensor_tensor(rank, rank, hot, ALU.mult)
            dve.drain()
            for k in (IN, OUT):
                dve.tensor_reduce(G.base_pos[:, k, 1, :], rank, AX.X, ALU.add)
            dve.drain()
            dve.tensor_copy(G.pos_i[:, :], G.base_pos[:, IN, 1, :])
            dve.tensor_copy(meta[:, :, 0], G.ids[:, :])
            dve.tensor_copy(meta[:, :, 1], G.degree[IN][:, :])
            dve.tensor_copy(meta[:, :, 2], G.degree[OUT][:, :])
            dve.memset(meta[:, :, 3], 0.0)
            dve.drain().then_inc(s_o.pos, 1)
            dve.tensor_scalar(tile_i, G.pos_i[:, :], 7, None, ALU.logical_shift_right)
            dve.tensor_scalar(low_i, G.pos_i[:, :], P - 1, None, ALU.bitwise_and)
            dve.drain()
            dve.tensor_copy(tile_f, tile_i)
            dve.tensor_copy(low_f, low_i)
            dve.drain()
            dve.tensor_tensor(tile_hot, bc(G.iota_row[:, 0:NT], 1, NT), bc(tile_f, 2, NT), ALU.is_equal)
            dve.wait_ge(s_o.load, 16)
            dve.tensor_copy(G.ids_i[:, :], G.by_pos[:, :, 0])
            dve.tensor_scalar(G.ids_in[:, :], G.by_pos[:, :, 0], float(G.N - 1), None, ALU.min)
            dve.wait_ge(s_o.tr, 1)
            for k in (IN, OUT):
                dve.tensor_reduce(kmax[0:NT, k:k + 1], G.banks[6][0:NT, k * P:(k + 1) * P], AX.X, ALU.max)
            dve.drain()
            for k in (IN, OUT):
                dve.memset(bnd[k][0:32, :], 0.0)
                dve.tensor_scalar(kmax[0:NT, k:k + 1], kmax[0:NT, k:k + 1], 1.0, None, ALU.max)
            dve.drain()
            for k in (IN, OUT):
                dve.tensor_copy(bnd[k][0:NT, 0:1], kmax[0:NT, k:k + 1])
                dve.tensor_scalar(t_i[0:NT, 2 * k:2 * k + 1], kmax[0:NT, k:k + 1], float(SLOTS - 1), None, ALU.add)
            dve.drain()
            for k in (IN, OUT):
                dve.tensor_scalar(t2_i[0:NT, 2 * k:2 * k + 1], t_i[0:NT, 2 * k:2 * k + 1], SHIFT, None,
                                  ALU.logical_shift_right)
            dve.drain()
            for k in (IN, OUT):
                dve.tensor_copy(bnd[k][0:NT, 1:2], t2_i[0:NT, 2 * k:2 * k + 1])
            dve.drain().then_inc(s_o.max, 1)
            dve.wait_ge(s_o.cum2, 1)
            for k in (IN, OUT):
                for col, q in ((2, 0), (3, 1)):
                    dve.tensor_copy(bnd[k][0:32, col:col + 1], G.banks[7][0:32, 8 * k + q:8 * k + q + 1])
            dve.drain()
            for k in (IN, OUT):
                dve.tensor_copy(bnd_i[k][0:32, :], bnd[k][0:32, :])
            dve.drain().then_inc(s_o.bnd, 1)
            dve.wait_ge(s_o.bld, 64)
            for k in (IN, OUT):
                dve.tensor_copy(first_f[k], first[k][:, 0:NT * HEADER].rearrange("p (n h) -> p n h", h=HEADER)[:, :, 2])
            dve.drain()
            for k in (IN, OUT):
                dve.tensor_tensor(picked, tile_hot, bc(first_f[k], 1, NT), ALU.mult)
                dve.drain()
                dve.tensor_reduce(G.base_pos[:, k, 0, :], picked, AX.X, ALU.add)
                dve.drain()
                dve.tensor_scalar(G.base_pos[:, k, 0, :], G.base_pos[:, k, 0, :], float(P), None, ALU.mult)
                dve.drain()
                dve.tensor_tensor(G.base_pos[:, k, 0, :], G.base_pos[:, k, 0, :], low_f, ALU.add)
                dve.drain()
                dve.tensor_scalar(G.base_pos[:, k, 0, :], G.base_pos[:, k, 0, :], float(SLOTS), None, ALU.mult)
                dve.drain()

        @block.tensor
        def _(pe):
            pe.wait_ge(s_o.hot, 1)
            pe.matmul(G.banks[5][:, 0:KEYS], lhsT=G.ones_bf[:, :], rhs=cum[:, NT, :],
                      start=True, stop=True).then_inc(s_o.count, 1)
            for g in range(NT // AG):
                out = G.banks[g][:, 0:AG * KEYS].rearrange("p (a k) -> p a k", k=KEYS)
                pe.matmul(out, lhsT=G.lower_bf[:, :], rhs=hot[:, g * AG:(g + 1) * AG, :], start=True, stop=False)
                pe.matmul(out, lhsT=G.ones_bf[:, :], rhs=cum[:, g * AG:(g + 1) * AG, :],
                          start=False, stop=True).then_inc(s_o.rank, 1)
            pe.wait_ge(s_o.load, 16)
            pe.transpose(G.banks[6][0:NT, 0:P], G.by_pos[:, :, 1], G.ident[:, :])
            pe.transpose(G.banks[6][0:NT, P:2 * P], G.by_pos[:, :, 2], G.ident[:, :]).then_inc(s_o.tr, 1)
            pe.wait_ge(s_o.max, 1)
            for k in (IN, OUT):
                for q, mask in enumerate((G.lower, G.same_parity)):
                    mm = pe.matmul(G.banks[7][0:32, 8 * k + q:8 * k + q + 1], lhsT=mask[0:NT, 0:32],
                                   rhs=bnd[k][0:NT, 1:2], start=(k == IN and q == 0), stop=True,
                                   skip_group_check=True)
            mm.then_inc(s_o.cum2, 1)

        @block.gpsimd
        def _(pool):
            pool.wait_ge(s_o.pos, 1)
            for a in range(NT):
                pool.indirect_dma_start(out=G.meta[:, :], out_offset=bass.IndirectOffsetOnAxis(
                    ap=G.pos_i[:, a:a + 1], axis=0), in_=meta[:, a, :], in_offset=None).then_inc(s_o.meta, 16)

        @block.sync
        def _(sp):
            sp.wait_ge(s_o.meta, 16 * NT)
            sp.dma_start(G.by_pos[:, :, :], G.meta.rearrange("(n p) q -> p n q", p=P)).then_inc(s_o.load, 16)
            sp.wait_ge(s_o.bnd, 1)
            for k in (IN, OUT):
                sp.dma_start(G.bounds_dram[k].rearrange("(n h) -> n h", h=HEADER), bnd_i[k][0:32, :]).then_inc(s_o.bst, 16)
            sp.wait_ge(s_o.bst, 32)
            for k in (IN, OUT):
                row = G.bounds_dram[k].rearrange("(o n) -> o n", o=1)
                sp.dma_start(G.bounds[k][:, :], row).then_inc(s_o.bld, 16)
                sp.dma_start(first[k], row.broadcast_to([P, 32 * HEADER])).then_inc(s_o.bld, 16)
            sp.wait_ge(s_o.bld, 64)


def scatter_edges(nc, M, G, arena):
    TA, NT, ET = TILES_AT_ONCE, G.NT, G.ET
    steps = ET // TA
    per_bank = 6
    assert per_bank * 3 * NT <= 512 and -(-TA // per_bank) == 3
    rows = G.MAX_ITEMS * P * SLOTS
    G.lists = [M.dram(f"lists{k}", [2 * rows, 2], I32) for k in (IN, OUT)]
    before = [b.rearrange("p (t a) -> p t a", a=NT) for b in G.before]
    row = [[arena(f"row{x}{k}", TA * P) for k in (IN, OUT)] for x in ("key", "lo")]
    lo_hot = [arena("lo_hot_in", TA * P), G.early[:, 0:TA * P]]
    hi_hot = arena("hi_hot_f", TA * NT).rearrange("p (t a) -> p t a", a=NT)
    looked = arena("looked", TA * 3 * NT).rearrange("p (t q a) -> p t q a", q=3, a=NT)
    value = [arena(f"value{k}", TA * 3).rearrange("p (t q) -> p t q", q=3) for k in (IN, OUT)]
    inside = [arena(f"inside{k}", TA) for k in (IN, OUT)]
    number = arena("number", TA)
    number_i, chunk_i, slot_i = (arena(x, TA, I32) for x in ("number_i", "chunk_i", "slot_i"))
    chunk_f, slot_f = arena("chunk_f", TA), arena("slot_f", TA)
    out_f = [arena(f"out_f{k}", TA) for k in (IN, OUT)]
    address = [[M.sb(f"address{k}_{x}", [P, TA], I32) for k in (IN, OUT)] for x in range(2)]
    entry = [[M.sb(f"entry{k}_{x}", [P, TA, 2], I32) for k in (IN, OUT)] for x in range(2)]
    assert steps % 2 == 1
    empty = M.sb("empty", [P, SLOTS, 2], I32)
    s_e = Named()
    s_e.empty = M.sem("s_e_empty")
    s_e.fill = M.sem("s_e_fill")
    s_e.rows_free = M.sem("s_e_rows_free")
    s_e.hot = M.sem("s_e_hot")
    s_e.look = M.sem("s_e_look")
    s_e.lread = M.sem("s_e_lread")
    s_e.entry = M.sem("s_e_entry")
    s_e.sent = M.sem("s_e_sent")
    scatter = [M.sem(f"s_e_scatter{x}") for x in range(2)]
    s_e.filled = M.sem("s_e_filled")
    s_e.seen = M.sem("s_e_seen")
    s_rows = [M.sem(f"s_e_rows{x}{k}") for x in range(2) for k in (IN, OUT)]
    with nc.Block() as block:

        @block.scalar
        def _(act):
            act.wait_ge(s_e.empty, 1)
            total = [act.value_load(G.bounds[k][0:1, NT * HEADER + 2:NT * HEADER + 3], min_val=NT,
                                   max_val=G.MAX_ITEMS) for k in (IN, OUT)]
            for k in (IN, OUT):
                with act.Fori(0, total[k]) as q:
                    act.dma_start(G.lists[k].rearrange("(q p s) c -> q p (s c)", p=P, s=SLOTS)[bass.ds(q, 1)].rearrange(
                        "q p s -> (q p) s"), empty[:, :, :].rearrange("p s c -> p (s c)")).then_inc(s_e.fill, 16)
            act.wait_ge(s_e.fill, (total[IN] + total[OUT]) * 16)
            act.sem_inc(s_e.filled, 1)

        @block.sync
        def _(sp):
            with sp.Fori(0, steps) as i:
                sp.wait_ge(s_e.rows_free, i + 1)
                for x in range(2):
                    for k in (IN, OUT):
                        sp.dma_start(row[x][k], G.key_rows[2 * x + k:2 * x + k + 1, bass.ds(i * (TA * P), TA * P)].broadcast_to(
                            [P, TA * P])).then_inc(s_rows[2 * x + k], 16)

        @block.vector
        def _(dve):
            dve.memset(empty[:, :, 0], G.PAD_ROW)
            dve.memset(empty[:, :, 1], 0)
            dve.drain().then_inc(s_e.empty, 1)
            dve.sem_inc(s_e.rows_free, 1)

            def step(i, x):
                for k in (IN, OUT):
                    dve.wait_ge(s_rows[2 + k], i * 16 + 16)
                    dve.wait_ge(s_e.look, i * 2 + (k + 1))
                    dve.tensor_scalar(lo_hot[k], row[1][k], G.iota_col[:, 0:1], None,
                                      ALU.is_equal).then_inc(s_e.hot, 1)
                for k in (IN, OUT):
                    dve.wait_ge(s_rows[k], i * 16 + 16)
                    for t in range(TA):
                        dve.scalar_tensor_tensor(out=row[0][k][:, t * P:(t + 1) * P], in0=row[0][k][:, t * P:(t + 1) * P],
                                                 scalar=G.key[k][:, bass.ds(i * TA + t, 1)], in1=G.upper[:, :],
                                                 op0=ALU.is_equal, op1=ALU.mult, accum_out=inside[k][:, t:t + 1])
                    dve.tensor_scalar(out_f[k], G.key[k][:, bass.ts(i, TA)], float(G.PAD_ROW), BIG,
                                      ALU.is_equal, ALU.mult)
                dve.drain()
                dve.sem_inc(s_e.rows_free, 1)
                for k in (IN, OUT):
                    dve.tensor_tensor(hi_hot, bc(G.iota_row[:, 0:NT], 1, TA),
                                      bc(G.hi[k][:, bass.ts(i, TA)], 2, NT), ALU.is_equal)
                    dve.drain()
                    dve.wait_ge(s_e.look, i * 2 + (k + 3))
                    for b in range(3):
                        n = min(per_bank, TA - b * per_bank)
                        got = G.banks[3 * k + b][:, 0:n * 3 * NT].rearrange("p (t q a) -> p t q a", q=3, a=NT)
                        for q in range(3):
                            ins = dve.tensor_tensor(looked[:, b * per_bank:b * per_bank + n, q, :], got[:, :, q, :],
                                                    hi_hot[:, b * per_bank:b * per_bank + n, :], ALU.mult)
                    ins.then_inc(s_e.lread, 1)
                    dve.drain()
                    dve.tensor_reduce(value[k], looked, AX.X, ALU.add)
                    dve.drain()
                    dve.tensor_tensor(number, value[k][:, :, 0], inside[k], ALU.add)
                    dve.drain()
                    dve.tensor_copy(number_i, number)
                    dve.drain()
                    dve.tensor_scalar(chunk_i, number_i, SHIFT, None, ALU.logical_shift_right)
                    dve.tensor_scalar(slot_i, number_i, SLOTS - 1, None, ALU.bitwise_and)
                    dve.drain()
                    dve.tensor_copy(chunk_f, chunk_i)
                    dve.tensor_copy(slot_f, slot_i)
                    dve.drain()
                    dve.scalar_tensor_tensor(out=number, in0=chunk_f, scalar=float(P * SLOTS), in1=slot_f,
                                             op0=ALU.mult, op1=ALU.add)
                    dve.tensor_tensor(out_f[k], out_f[k], value[k][:, :, 1], ALU.add)
                    dve.drain()
                    if k == IN:
                        dve.wait_ge(s_e.sent, i + 1)
                    dve.tensor_tensor(address[x][k][:, :], number, out_f[k], ALU.add)
                    dve.drain()
                for k in (IN, OUT):
                    dve.tensor_copy(entry[x][k][:, :, 0], value[1 - k][:, :, 2])
                    dve.tensor_copy(entry[x][k][:, :, 1].bitcast(F32), G.w[:, bass.ts(i, TA)])
                dve.drain().then_inc(s_e.entry, 1)

            step(0, 0)
            with dve.Fori(0, steps // 2) as j:
                step(j * 2 + 1, 1)
                step(j * 2 + 2, 0)

        @block.tensor
        def _(pe):
            pe.sem_inc(s_e.look, 2)
            pe.sem_inc(s_e.lread, 2)
            with pe.Fori(0, steps) as i:
                for k in (IN, OUT):
                    pe.wait_ge(s_e.hot, i * 2 + (k + 1))
                    pe.wait_ge(s_e.lread, i * 2 + (k + 1))
                    for t in range(TA):
                        at = G.banks[3 * k + t // per_bank][:, (t % per_bank) * 3 * NT:(t % per_bank + 1) * 3 * NT]
                        pe.matmul(at[:, 0:NT], lhsT=lo_hot[k][:, t * P:(t + 1) * P],
                                  rhs=before[k][:, bass.ds(i * TA + t, 1), :].rearrange("p o a -> p (o a)"),
                                  start=(t % per_bank == 0), stop=True, skip_group_check=True)
                        mm = pe.matmul(at[:, NT:3 * NT], lhsT=lo_hot[k][:, t * P:(t + 1) * P],
                                       rhs=G.base_pos[:, k, :, :].rearrange("p q a -> p (q a)"),
                                       start=False, stop=True, skip_group_check=True)
                    mm.then_inc(s_e.look, 1)

        @block.gpsimd
        def _(pool):
            pool.sem_inc(s_e.sent, 2)
            pool.wait_ge(s_e.filled, 1)
            last_row = pool.to_reg(rows - 1)

            def step(i, x, j):
                pool.wait_ge(s_e.entry, i + 1)
                pool.sem_inc(s_e.seen, 1)
                for t in range(TA):
                    if t == TA // 2 and j is not None:
                        pool.wait_ge(scatter[1 - x], j * (2 * 16 * TA) + 2 * 16 * TA)
                        pool.sem_inc(s_e.sent, 1)
                    for k in (IN, OUT):
                        pool.indirect_dma_start(out=G.lists[k][:, :], out_offset=bass.IndirectOffsetOnAxis(
                            ap=address[x][k][:, t:t + 1], axis=0), in_=entry[x][k][:, t, :], in_offset=None,
                            bounds_check=last_row, oob_is_err=False).then_inc(scatter[x], 16)

            step(0, 0, None)
            with pool.Fori(0, steps // 2) as j:
                step(j * 2 + 1, 1, j)
                step(j * 2 + 2, 0, j)
            for x in range(2):
                pool.wait_ge(scatter[x], (steps + 1 - x) // 2 * 2 * 16 * TA)


def weights(nc, M, G, a):
    G.x_all = G.store[:, 0:G.NT * 256].rearrange("p (n f) -> p n f", f=256)
    G.x = [M.dram(f"x{j}", [G.ROWS, 256]) for j in range(4)]
    s_x, s_xs = M.sem("s_x"), M.sem("s_xs")
    H1, C1 = 4, 128
    G.W1 = G.early[:, 0:2 * 520].rearrange("p (k n) -> p k n", k=2)
    G.W2 = G.early[:, 2 * 520:2 * 520 + 4 * 258].rearrange("p (k n) -> p k n", k=4)
    G.W3 = M.sb("W3", [P, 2, 260])
    G.W4 = M.sb("W4", [P, 2, 256])
    G.W5 = M.sb("W5", [P, 2, 256])
    G.W6 = M.sb("W6", [P, 2, 512])
    G.row3 = M.sb("row3", [1, 260])
    G.row6 = M.sb("row6", [1, 512])
    G.b1 = M.sb("b1", [P, 512])
    G.b2 = M.sb("b2", [P, 256])
    G.b4 = M.sb("b4", [P, 256])
    G.b5 = M.sb("b5", [P, 256])
    G.slope = M.sb("slope", [P, 1])
    store, at = G.store, [G.arena_at]

    def tmp(n):
        at[0] += n
        return store[:, at[0] - n:at[0]]

    as1, ad1, as2, ad2, a3 = tmp(512), tmp(512), tmp(256), tmp(256), tmp(256)
    th, ph = tmp(512).rearrange("p (k n) -> p k n", k=2), tmp(512).rearrange("p (k n) -> p k n", k=2)
    rb = tmp(512)
    junk = tmp(40 * 128).rearrange("p (j n) -> p j n", n=128)
    junk2 = tmp(8 * 256).rearrange("p (j n) -> p j n", n=256)
    zero, lowest = tmp(520), tmp(256)
    G.tables = [M.dram(f"table{j}", [G.ROWS, w]) for j, w in enumerate((520, 258, 260, 256, 256, 256))]
    G.own6 = M.dram("own6", [G.ROWS, 256])
    s_w, s_d, s_t, s_z, s_zd = M.sem("s_w"), M.sem("s_wd"), M.sem("s_wt"), M.sem("s_wz"), M.sem("s_wzd")

    def row(x):
        return x.rearrange("(o n) -> o n", o=1)

    with nc.Block() as block:

        @block.sync
        def _(sp):
            loads = [
                (G.W1[:, :, 0:512], a.W1.rearrange("(k p) n -> p k n", p=P)),
                (G.W2[:, :, 0:256], a.W2.rearrange("(k p) n -> p k n", p=P)),
                (G.W3[:, :, 0:256], a.W3.rearrange("(k p) n -> p k n", p=P)),
                (G.W4[:, :, :], a.W4.rearrange("(k p) n -> p k n", p=P)),
                (G.W5[:, :, :], a.W5.rearrange("(k p) n -> p k n", p=P)),
                (th, a.theta.rearrange("(k p) n -> p k n", p=P)),
                (ph, a.phi.rearrange("(k p) n -> p k n", p=P)),
                (as1, a.as1.rearrange("(o h) c -> o (h c)", o=1).broadcast_to([P, 512])),
                (ad1, a.ad1.rearrange("(o h) c -> o (h c)", o=1).broadcast_to([P, 512])),
                (as2, a.as2.broadcast_to([P, 256])),
                (ad2, a.ad2.broadcast_to([P, 256])),
                (a3, row(a.a3).broadcast_to([P, 256])),
                (G.b1[:, :], row(a.b1).broadcast_to([P, 512])),
                (G.b2[:, :], row(a.b2).broadcast_to([P, 256])),
                (G.b4[:, :], row(a.b4).broadcast_to([P, 256])),
                (G.b5[:, :], row(a.b5).broadcast_to([P, 256])),
                (G.slope[:, :], a.slope.broadcast_to([P, 1])),
                (G.row3[0:1, 0:256], row(a.b3)),
                (G.row6[0:1, 256:512], row(a.theta_b)),
                (rb[0:1, 0:256], row(a.phi_b)),
            ]
            for dst, src in loads:
                sp.dma_start(dst, src).then_inc(s_w, 16)
            sp.wait_ge(s_z, 1)
            for j, t in enumerate(G.tables):
                empty = lowest if j == len(G.tables) - 1 else zero
                sp.dma_start(t[G.PAD_ROW:G.PAD_ROW + 1, :], empty[0:1, 0:t.shape[1]]).then_inc(s_zd, 16)
            sp.wait_ge(s_zd, 16 * len(G.tables))
        NL = 20

        @block.vector
        def _(dve):
            dve.memset(zero[0:1, :], 0.0)
            dve.memset(lowest[0:1, :], LOWEST)
            dve.memset(G.row6[0:1, 0:256], 0.0)
            dve.drain().then_inc(s_z, 1)
            dve.wait_ge(s_w, 16 * NL)
            j = 0
            for k in range(2):
                for h in range(H1):
                    for v, vec in ((0, as1), (4, ad1)):
                        cols = slice(h * C1, (h + 1) * C1)
                        dve.tensor_tensor_reduce(junk[:, j, :], G.W1[:, k, cols], vec[:, cols], 1.0, 0.0,
                                                 ALU.mult, ALU.add, G.W1[:, k, 512 + v + h:513 + v + h])
                        j += 1
            for k in range(4):
                for v, vec in ((0, as2), (1, ad2)):
                    dve.tensor_tensor_reduce(junk2[:, 2 * k + v, :], G.W2[:, k, 0:256], vec, 1.0, 0.0,
                                             ALU.mult, ALU.add, G.W2[:, k, 256 + v:257 + v])
            for k in range(3):
                src, n = (G.W3[:, k, :], P) if k < 2 else (G.row3[:, :], 1)
                for h in range(2):
                    for v in range(2):
                        dve.tensor_tensor_reduce(junk[0:n, j, :], src[:, h * P:(h + 1) * P],
                                                 a3[0:n, (1 - v) * P:(2 - v) * P], 1.0, 0.0, ALU.mult, ALU.add,
                                                 src[:, 256 + 2 * v + h:257 + 2 * v + h])
                        j += 1
            dve.tensor_tensor(ph, ph, th, ALU.subtract)
            dve.tensor_tensor(G.row6[0:1, 256:512], G.row6[0:1, 256:512], rb[0:1, 0:256], ALU.add)
            dve.drain().then_inc(s_d, 1)
            dve.wait_ge(s_t, 1)
            for v in range(2):
                for k in range(2):
                    dve.tensor_copy(G.W6[:, k, v * 256:(v + 1) * 256],
                                    G.banks[v][:, k * 256:(k + 1) * 256])

        @block.tensor
        def _(pe):
            pe.wait_ge(s_d, 1)
            for v, x in enumerate((ph, th)):
                for k in range(2):
                    for o in range(2):
                        mm = pe.transpose(G.banks[v][:, k * 256 + o * P:k * 256 + (o + 1) * P],
                                          x[:, o, k * P:(k + 1) * P], G.ident[:, :])
            mm.then_inc(s_t, 1)

        @block.gpsimd
        def _(pool):
            for n in range(G.NT):
                pool.indirect_dma_start(out=G.x_all[:, n, :], out_offset=None, in_=a.x,
                                        in_offset=bass.IndirectOffsetOnAxis(ap=G.ids_in[:, n:n + 1], axis=0)
                                        ).then_inc(s_x, 16)

        @block.scalar
        def _(act):
            act.wait_ge(s_x, 16 * G.NT)
            act.dma_start(G.x[0][0:G.PAD_ROW].rearrange("(n p) f -> p n f", p=P), G.x_all).then_inc(s_xs, 16)
            act.wait_ge(s_xs, 16)


class Layer:

    def __init__(self, name, kind, lst, heads, width, row, table=None, own_from=None, x_in=None, x_out=None,
                 self_loop=True, norm=False, norm_of=None, sum_weights=False, scale_out=False, stores=(),
                 weight=None, bias_row=None, depth=0, out_width=0, finish=None, out=None):
        self.name, self.kind, self.list = name, kind, lst
        self.heads, self.width = heads, width
        self.row, self.own_width = row, row
        self.table, self.own_from = table, own_from
        self.x_in, self.x_out = x_in, x_out
        self.self_loop = self_loop
        self.norm, self.norm_of = norm, norm_of
        self.sum_weights = sum_weights
        self.scale_out = scale_out
        self.stores = stores
        self.weight, self.bias_row, self.depth, self.out_width = weight, bias_row, depth, out_width
        self.finish = finish or finish_none
        self.out = out


def layer(nc, M, G, L):
    NT = G.NT
    kind, k = L.kind, L.list
    H, F, R = L.heads, L.width, L.row
    HD = F // H
    gat, gcn, mx, pre = kind == "gat", kind == "gcn", kind == "max", kind == "pre"
    name = L.name
    sem = lambda x: M.sem(f"{name}_{x}")
    S = Named()
    S.logits, S.probs, S.diag, S.group, S.corr = sem("logits"), sem("probs"), sem("diag"), sem("group"), sem("corr")
    S.sums, S.evac, S.acc = sem("sums"), sem("evac"), sem("acc")
    S.z, S.var, S.dev, S.turned, S.zt = sem("z"), sem("var"), sem("dev"), sem("turned"), sem("zt")
    S.wide, S.row, S.stored = sem("wide"), sem("row"), sem("stored")
    S.mark, S.out = sem("mark"), sem("out")
    listed, rows, free, own_in, x_here, st = ([sem(f"{x}{b}") for b in range(2)] for x in
                                              ("listed", "rows", "free", "own", "x", "st"))
    sums = G.banks[0]
    turned = G.banks[1]
    wide = [G.banks[2], G.banks[3]]
    per_gather = GROUP if mx else 2
    if not pre:
        gbuf = G.store[:, 0:2 * SLOTS * R].rearrange("p (b s r) -> p b s r", b=2, s=SLOTS)
        lst = [G.lst[:, b, :, :] for b in range(2)]
        own = [G.own[:, b, 0:L.own_width] for b in range(2)]
        diag = [G.work[:, j * 16 * P:j * 16 * P + H * GROUP * P].rearrange("p (h s m) -> p h s m", h=H, m=P)
                for j in range(2)]
        corr = G.corr[:, 0:H * P].rearrange("p (h m) -> p h m", m=P)
        logits = G.logits[:, 0:H, :]
        probs = G.probs[:, 0:H, :]
        lists = G.lists[k].rearrange("(q p s) c -> q p (s c)", p=P, s=SLOTS)
    KT, WD = L.depth, L.out_width
    has_store_x = L.x_out is not None
    count = len(L.stores) + has_store_x
    late_row = gat and not L.scale_out
    own_late = mx or not L.self_loop

    class Counts:

        def __init__(self, eng):
            self.eng = eng

            def register(x):
                r = eng.alloc_register(f"{name}_{x}")
                eng.reg_mov(r, 0)
                return r

            self.tmp, self.end = register("tmp"), register("end")
            self.before = register("before")
            self.last = register("last")
            self.same = [register(f"same{b}") for b in range(2)]
            self.groups = register("groups")
            self.landed = [register(f"landed{b}") for b in range(2)]

        def add(self, reg, v):
            self.eng.reg_alu(reg, reg, v, ALU.add)

        def wait(self, semaphore, reg, v, times=1):
            self.eng.reg_mov(self.tmp, v)
            self.eng.reg_alu(self.tmp, self.tmp, reg, ALU.add)
            if times > 1:
                self.eng.reg_alu(self.tmp, self.tmp, times, ALU.mult)
            self.eng.wait_ge(semaphore, self.tmp)

        def rows_until(self, b, K):
            shift = 2 if per_gather == 4 else 1
            self.eng.reg_mov(self.end, K + (per_gather - 1))
            self.eng.reg_alu(self.end, self.end, shift, ALU.logical_shift_right)
            self.eng.reg_alu(self.end, self.end, per_gather, ALU.mult)
            self.eng.reg_alu(self.end, self.end, self.landed[b], ALU.add)

        def wait_rows(self, b, c):
            self.eng.reg_mov(self.tmp, c * SLOTS + SLOTS)
            self.eng.reg_alu(self.tmp, self.tmp, self.landed[b], ALU.add)
            self.eng.reg_alu(self.tmp, self.tmp, self.end, ALU.min)
            self.eng.reg_alu(self.tmp, self.tmp, 16, ALU.mult)
            self.eng.wait_ge(rows[b], self.tmp)

        def tile_done(self, b, chunks, gathered=False):
            self.eng.reg_mov(self.last, self.before)
            self.add(self.before, chunks)
            self.add(self.same[b], chunks)
            if gathered:
                self.eng.reg_mov(self.landed[b], self.end)

    def bounds(eng, n, *which):
        ranges = ((1, G.E), (1, G.MAX_ITEMS), (0, G.MAX_ITEMS), (0, G.MAX_ITEMS))
        return [eng.value_load(G.bounds[k][0:1, bass.ds(n * HEADER + j, 1)], min_val=ranges[j][0],
                               max_val=ranges[j][1]) for j in which]

    def walk(eng, agg, post, within=None):
        pairs = (NT - 1) // 2
        assert NT == 2 * pairs + 1
        if pre:
            with eng.Fori(0, pairs) as i:
                post(i * 2, 0, i)
                post(i * 2 + 1, 1, i)
            post(NT - 1, 0, pairs)
            return
        agg(0, 0, 0)
        if within:
            with eng.Fori(0, pairs) as i:
                agg(i * 2 + 1, 1, i, lambda: within(i * 2, 0, i))
                if post is not within:
                    post(i * 2, 0, i)
                agg(i * 2 + 2, 0, i + 1, lambda: within(i * 2 + 1, 1, i))
                if post is not within:
                    post(i * 2 + 1, 1, i)
            if post is not within:
                within(NT - 1, 0, pairs)
            post(NT - 1, 0, pairs)
            return
        with eng.Fori(0, pairs) as i:
            agg(i * 2 + 1, 1, i)
            post(i * 2, 0, i)
            agg(i * 2 + 2, 0, i + 1)
            post(i * 2 + 1, 1, i)
        post(NT - 1, 0, pairs)

    with nc.Block() as block:

        @block.gpsimd
        def _(pool):
            if pre:
                pool.memset(G.store[:, NT * 256:], 0.0)
                return

            counts = Counts(pool)

            def agg(n, b, t):
                K, chunks = bounds(pool, n, 0, 1)
                with pool.Fori(0, chunks) as c:
                    counts.wait(listed[b], counts.same[b], c + 1, 16)
                    pool.sem_inc(S.mark, 1)
                    for j in range(0, SLOTS, per_gather):
                        with pool.If(K - c * SLOTS > j):
                            for s in range(j, j + per_gather):
                                pool.indirect_dma_start(
                                    out=gbuf[:, b, s, :], out_offset=None, in_=L.table[0:G.PAD_ROW + 1, :],
                                    in_offset=bass.IndirectOffsetOnAxis(ap=lst[b][:, s, 0:1], axis=0)
                                ).then_inc(rows[b], 16)
                counts.tile_done(b, chunks)

            def scatter(n, b):
                pool.wait_ge(S.z, n + 1)
                pool.sem_inc(S.mark, 1)
                pool.indirect_dma_start(out=L.out, out_offset=bass.IndirectOffsetOnAxis(ap=G.ids_t[:, b:b + 1], axis=0),
                                        in_=G.xn[:, b, :], in_offset=None, bounds_check=last_node,
                                        oob_is_err=False).then_inc(S.out, 16)

            def scattered(n):
                pool.wait_ge(S.out, n * 16 + 16)
                pool.sem_inc(S.stored, 1)

            if not mx:
                agg(0, 0, 0)
                with pool.Fori(0, (NT - 1) // 2) as i:
                    agg(i * 2 + 1, 1, i)
                    agg(i * 2 + 2, 0, i)
            else:
                last_node = pool.to_reg(G.N - 1)
                pool.sem_inc(S.stored, 2)
                agg(0, 0, 0)
                agg(1, 1, 0)
                agg(2, 0, 0)
                scatter(0, 0)
                with pool.Fori(0, (NT - 3) // 2) as i:
                    agg(i * 2 + 3, 1, i)
                    scattered(i * 2)
                    scatter(i * 2 + 1, 1)
                    agg(i * 2 + 4, 0, i)
                    scattered(i * 2 + 1)
                    scatter(i * 2 + 2, 0)
                for n in (NT - 2, NT - 1):
                    scattered(n - 1)
                    scatter(n, n % 2)
                scattered(NT - 1)

        @block.sync
        def _(sp):
            def agg(n, b, earlier=None):
                if isinstance(n, int) and n == 0:
                    (chunks,), before, same = bounds(sp, n, 1), 0, 0
                elif isinstance(n, int) and n == 1:
                    (chunks, before), same = bounds(sp, n, 1, 2), 0
                else:
                    chunks, before, same = bounds(sp, n, 1, 2, 3)

                def one(c):
                    sp.wait_ge(free[b], same + c + 1)
                    sp.dma_start(lst[b].rearrange("p s c -> p (s c)"),
                                 lists[bass.ds(before + c, 1)].rearrange("q p s -> (q p) s")).then_inc(listed[b], 16)

                one(0)
                if earlier is not None:
                    put(earlier, 1 - b)
                with sp.If(chunks > 1):
                    with sp.Fori(0, chunks - 1) as c:
                        one(c + 1)

            def load_x(n, b):
                sp.dma_start(G.xt[:, b, :], L.x_in[bass.ds(n * P, P), :]).then_inc(x_here[b], 16)

            def put(n, b, more=True):
                if mx:
                    return
                if has_store_x:
                    sp.wait_ge(S.z, n + 1)
                    sp.dma_start(L.x_out[bass.ds(n * P, P), :], G.xn[:, b, :]).then_inc(st[b], 16)
                    if more:
                        load_x(n + 2, b)
                sp.wait_ge(S.row, n + 2)
                for to, lo, hi in L.stores:
                    sp.dma_start(to[bass.ds(n * P, P), :], G.row[:, b, lo:hi]).then_inc(st[b], 16)

            if pre:
                with sp.Fori(0, (NT - 1) // 2) as i:
                    put(i * 2, 0)
                    put(i * 2 + 1, 1)
                put(NT - 1, 0)
            else:
                for b in range(2):
                    agg(b, b)
                    if has_store_x:
                        load_x(b, b)
                agg(2, 0)
                with sp.Fori(0, (NT - 3) // 2) as i:
                    agg(i * 2 + 3, 1, i * 2)
                    agg(i * 2 + 4, 0, i * 2 + 1)
                put(NT - 3, 0)
                put(NT - 2, 1, more=False)
                put(NT - 1, 0, more=False)
            if not mx:
                for b in range(2):
                    sp.wait_ge(st[b], ((NT + 1 - b) // 2 + 1) * 16 * count)

        @block.scalar
        def _(act):
            counts = Counts(act)

            def load_own(n, b):
                act.dma_start(own[b], L.own_from[bass.ds(n * P, P), :]).then_inc(own_in[b], 16)

            def load_x(n, b):
                act.dma_start(G.xt[:, b, :], L.x_in[bass.ds(n * P, P), :]).then_inc(x_here[b], 16)

            def start_acc(n, b, t):
                act.wait_ge(own_in[b], t * 16 + 16)
                act.copy(G.acc[:, b, 0:F], own[b][:, 0:F]).then_inc(S.acc, 1)

            def own_of_next(n, b, t):
                if own_late:
                    return
                if isinstance(n, int):
                    load_own(n + 2, b)
                else:
                    with act.If(t < (NT - 1) // 2 - b):
                        load_own(n + 2, b)

            def agg(n, b, t, last_tile=None):
                chunks, = bounds(act, n, 1)
                if mx:
                    return None
                with act.Fori(0, chunks) as c:
                    if gat:
                        counts.wait(S.logits, counts.before, c + 1)
                        act.activation(probs, logits, ACT.Exp).then_inc(S.probs, 1)
                        if last_tile is not None:
                            with act.If(c < 1):
                                last_tile()
                    counts.wait(S.sums, counts.before, c + 2)
                    act.copy(G.acc[:, b, 0:F], sums[:, 0:F]).then_inc(S.evac, 1)
                    act.drain().then_inc(free[b], 1)
                counts.tile_done(b, chunks)
                own_of_next(n, b, t)

            def root(n, b, t):
                act.wait_ge(S.var, n + 1)
                act.activation(G.dev[:, :], G.mv[:, 1:2], ACT.Sqrt).then_inc(S.dev, 1)

            def within(n, b, t):
                if late_row:
                    if b == 0 and not isinstance(n, int):
                        with act.If(t > 0):
                            row_out(n, 1, t)
                    else:
                        row_out(n, 1 - b, t + b)
                if L.norm:
                    root(n, b, t)

            def post(n, b, t):
                if L.norm and not gat and not pre:
                    root(n, b, t)
                if not pre:
                    load_next(n, b, t)
                if mx:
                    return
                act.wait_ge(S.turned, n + 2)
                if L.norm:
                    act.activation(G.zt[:, 0:KT * P], turned[:, 0:KT * P], ACT.Relu).then_inc(S.zt, 1)
                else:
                    act.copy(G.zt[:, 0:KT * P], turned[:, 0:KT * P]).then_inc(S.zt, 1)
                if L.self_loop and not pre and not isinstance(n, int):
                    if b == 0:
                        start_acc(n + 2, b, t + 1)
                    else:
                        with act.If(t < (NT - 1) // 2 - 1):
                            start_acc(n + 2, b, t + 1)
                if not late_row:
                    row_out(n + 1, b, t + 1, G.dinv[:, bass.ds(n, 1)] if L.scale_out else None)

            def row_out(tiles, b, turn, scale=None):
                act.wait_ge(S.wide, tiles)
                act.wait_ge(st[b], turn * (16 * count))
                if L.scale_out:
                    act.activation(G.row[:, b, 0:min(WD, 512)], wide[0][:, 0:min(WD, 512)], ACT.Copy, scale=scale)
                else:
                    act.copy(G.row[:, b, 0:min(WD, 512)], wide[0][:, 0:min(WD, 512)])
                if WD > 512:
                    act.copy(G.row[:, b, 512:WD], wide[1][:, 0:WD - 512])
                act.drain().then_inc(S.row, 1)

            def load_next(n, b, t):
                if not own_late or isinstance(n, int):
                    return

                def load():
                    act.wait_ge(S.z, n + 1)
                    load_own(n + 2, b)
                    if mx:
                        load_x(n + 2, b)

                if b == 0:
                    load()
                else:
                    with act.If(t < (NT - 1) // 2 - 1):
                        load()

            if not pre:
                for b in range(2):
                    load_own(b, b)
                    if mx:
                        load_x(b, b)
                if L.self_loop and not mx:
                    for b in range(2):
                        start_acc(b, b, 0)
                act.sem_inc(S.evac, 1)
                for b in range(2):
                    act.sem_inc(free[b], 1)
            act.sem_inc(S.zt, 1)
            act.sem_inc(S.row, 1)
            if not mx:
                for b in range(2):
                    act.sem_inc(st[b], 16 * count)
            if pre:
                act.wait_ge(S.var, 1)
                act.activation(G.root_all[:, :], G.root_all[:, :], ACT.Sqrt).then_inc(S.dev, 1)
            walk(act, agg, post, within if gat else None)
            if late_row:
                row_out(NT, 0, (NT + 1) // 2)

        @block.tensor
        def _(pe):
            counts = Counts(pe)

            def agg(n, b, t):
                if mx:
                    return
                K, chunks = bounds(pe, n, 0, 1)
                if gcn:
                    counts.rows_until(b, K)
                with pe.Fori(0, chunks) as c:
                    if gcn:
                        counts.wait_rows(b, c)
                    counts.wait(S.evac, counts.before, c + 1)
                    for g in range(NGROUP):
                        with pe.If(K - c * SLOTS > g * GROUP):
                            counts.wait(S.diag, counts.groups, 1)
                            counts.add(counts.groups, 1)
                            for s in range(GROUP):
                                for h in range(H):
                                    mm = pe.matmul(sums[:, h * HD:(h + 1) * HD], lhsT=diag[g % 2][:, h, s, :],
                                                   rhs=gbuf[:, b, g * GROUP + s, h * HD:(h + 1) * HD],
                                                   start=(g == 0 and s == 0 and h == 0), stop=True,
                                                   skip_group_check=True)
                            mm.then_inc(S.group, 1)
                    pe.wait_ge(S.acc, n + 1)
                    if gat:
                        counts.wait(S.corr, counts.before, c + 1)
                    for h in range(H):
                        mm = pe.matmul(sums[:, h * HD:(h + 1) * HD], lhsT=corr[:, h, :] if gat else G.ident[:, :],
                                       rhs=G.acc[:, b, h * HD:(h + 1) * HD], start=False, stop=True,
                                       skip_group_check=True)
                    mm.then_inc(S.sums, 1)
                counts.tile_done(b, chunks, gcn)

            def post(n, b, t):
                if mx:
                    return
                pe.wait_ge(S.z, n + 1)
                pe.wait_ge(S.zt, n + 1)
                for j in range(KT):
                    mm = pe.transpose(turned[:, j * P:(j + 1) * P], G.z[:, j * P:(j + 1) * P], G.ident[:, :])
                mm.then_inc(S.turned, 1)
                pe.wait_ge(S.zt, n + 2)
                pe.wait_ge(S.row, n + 1)
                for lo in range(0, WD, 512):
                    hi = min(WD, lo + 512)
                    out = wide[lo // 512][:, 0:hi - lo]
                    for j in range(KT):
                        mm = pe.matmul(out, lhsT=G.zt[:, j * P:(j + 1) * P], rhs=L.weight[:, j, lo:hi],
                                       start=(j == 0), stop=(j == KT - 1 and L.bias_row is None))
                    if L.bias_row is not None:
                        mm = pe.matmul(out, lhsT=G.one_row[:, :], rhs=L.bias_row[:, lo:hi], start=False, stop=True)
                mm.then_inc(S.wide, 1)

            if not pre:
                pe.sem_inc(S.group, 2)
                pe.sem_inc(S.sums, 1)
            pe.sem_inc(S.turned, 1)
            walk(pe, agg, post)

        @block.vector
        def _(dve):
            counts = Counts(dve)

            def agg(n, b, t, last_tile=None):
                K, chunks = bounds(dve, n, 0, 1)
                if gat or mx:
                    counts.rows_until(b, K)
                gb = gbuf[:, b, :, :]
                m, den = G.m[:, b, 0:H], G.den[:, b, 0:H]
                if not gcn:
                    dve.wait_ge(own_in[b], (t + 1) * 16)
                if gat:
                    if L.self_loop:
                        dve.tensor_tensor(m, own[b][:, F:F + H], own[b][:, F + H:F + 2 * H], ALU.add)
                        dve.drain()
                        dve.scalar_tensor_tensor(out=m, in0=m, scalar=SLOPE, in1=m, op0=ALU.mult, op1=ALU.max)
                        dve.memset(den, 1.0)
                    else:
                        dve.memset(m, NEG)
                        dve.memset(den, 0.0)
                        dve.memset(G.acc[:, b, 0:F], 0.0).then_inc(S.acc, 1)
                elif mx:
                    dve.memset(G.acc[:, b, 0:F], LOWEST)
                if L.sum_weights:
                    dve.memset(G.wsum[:, :], 1.0)
                if not gcn:
                    dve.drain()
                with dve.Fori(0, chunks) as c:
                    counts.wait(listed[b], counts.same[b], c + 1, 16)
                    if L.sum_weights:
                        dve.tensor_reduce(G.wpart[:, :], lst[b][:, :, 1].bitcast(F32), AX.X, ALU.add)
                    if gat:
                        dve.tensor_scalar(G.mask[:, :], lst[b][:, :, 0], float(G.PAD_ROW), NEG, ALU.is_equal, ALU.mult)
                    if gat or mx:
                        counts.wait_rows(b, c)
                    if gat:
                        lg = logits[:, :, 0:SLOTS]
                        dve.tensor_tensor(lg, gb[:, :, F:F + H].rearrange("p s h -> p h s"),
                                          bc(own[b][:, F + H:F + 2 * H], 2, SLOTS), ALU.add)
                        dve.drain()
                        if L.sum_weights:
                            dve.tensor_tensor(G.wsum[:, :], G.wsum[:, :], G.wpart[:, :], ALU.add)
                        dve.scalar_tensor_tensor(out=lg, in0=lg, scalar=SLOPE, in1=lg, op0=ALU.mult, op1=ALU.max)
                        dve.drain()
                        dve.tensor_tensor(lg, lg, bc(G.mask[:, :], 1, H), ALU.add)
                        dve.drain()
                        dve.tensor_reduce(G.mnew[:, 0:H], lg, AX.X, ALU.max)
                        dve.drain()
                        dve.tensor_tensor(G.mnew[:, 0:H], G.mnew[:, 0:H], m, ALU.max)
                        dve.drain()
                        dve.tensor_tensor(lg, lg, bc(G.mnew[:, 0:H], 2, SLOTS), ALU.subtract)
                        dve.tensor_tensor(logits[:, :, SLOTS], m, G.mnew[:, 0:H], ALU.subtract)
                        dve.drain().then_inc(S.logits, 1)
                        dve.tensor_copy(m, G.mnew[:, 0:H])
                        counts.wait(S.probs, counts.before, c + 1)
                        dve.tensor_tensor(den, den, probs[:, :, SLOTS], ALU.mult)
                        dve.tensor_reduce(G.dsum[:, 0:H], probs[:, :, 0:SLOTS], AX.X, ALU.add)
                        dve.drain()
                        dve.tensor_tensor(den, den, G.dsum[:, 0:H], ALU.add)
                    if gat or gcn:
                        for g in range(NGROUP):
                            with dve.If(K - c * SLOTS > g * GROUP):
                                counts.wait(S.group, counts.groups, 1 + (g == 0))
                                counts.add(counts.groups, 1)
                                if gat:
                                    wts = probs[:, :, g * GROUP:(g + 1) * GROUP]
                                else:
                                    wts = lst[b][:, g * GROUP:(g + 1) * GROUP, 1].bitcast(F32).unsqueeze(1)
                                dve.tensor_tensor(diag[g % 2].rearrange("p h s m -> p (h s) m"),
                                                  bc(G.ident[:, :], 1, H * GROUP),
                                                  bc(wts, 3, P).rearrange("p h s m -> p (h s) m") if H == 1 else
                                                  bc(wts, 3, P), ALU.mult).then_inc(S.diag, 1)
                            if g == 1 and last_tile is not None:
                                with dve.If(c < 1):
                                    last_tile()
                        if gat:
                            counts.wait(S.sums, counts.before, c + 1)
                            dve.tensor_tensor(corr, bc(G.ident[:, :], 1, H), bc(probs[:, :, SLOTS], 2, P),
                                              ALU.mult).then_inc(S.corr, 1)
                    if mx:
                        for g in range(NGROUP):
                            with dve.If(K - c * SLOTS > g * GROUP):
                                dve.tensor_reduce(G.part[:, g, :], gb[:, g * GROUP:(g + 1) * GROUP, :].rearrange(
                                    "p s f -> p f s"), AX.X, ALU.max)
                            with dve.Else():
                                dve.memset(G.part[:, g, :], LOWEST)
                        dve.drain().then_inc(free[b], 1)
                        dve.tensor_reduce(G.z[:, 0:F], G.part.rearrange("p g f -> p f g"), AX.X, ALU.max)
                        dve.drain()
                        dve.tensor_tensor(G.acc[:, b, 0:F], G.acc[:, b, 0:F], G.z[:, 0:F], ALU.max)
                        dve.drain()
                if L.sum_weights:
                    dve.drain()
                    dve.tensor_copy(G.wdeg[:, bass.ds(n, 1)], G.wsum[:, :])
                counts.tile_done(b, chunks, not gcn)

            def post(n, b, t):
                acc, xn, xt, z = G.acc[:, b, :], G.xn[:, b, :], G.xt[:, b, :], G.z
                if not pre:
                    if not mx:
                        counts.wait(S.evac, counts.before if gat or isinstance(n, int) else counts.last, 1)
                    if gat:
                        dve.reciprocal(G.rden[:, 0:H], G.den[:, b, 0:H])
                        if not L.self_loop:
                            dve.tensor_scalar(G.some[:, 0:H], G.m[:, b, 0:H], NEG * 0.1, None, ALU.is_gt)
                            dve.tensor_scalar(G.none[:, 0:H], G.m[:, b, 0:H], NEG * 0.1, None, ALU.is_le)
                        dve.drain()
                        if not L.self_loop:
                            dve.tensor_tensor(G.rden[:, 0:H], G.rden[:, 0:H], G.some[:, 0:H], ALU.mult)
                            dve.drain()
                if L.x_in is not None:
                    dve.wait_ge(x_here[b], t * 16 + 16)
                if has_store_x:
                    dve.wait_ge(st[b], t * (16 * count) + 16 * count)
                elif mx:
                    dve.wait_ge(S.stored, n + 1)
                if mx:
                    dve.tensor_copy(G.ids_t[:, b:b + 1], G.ids_i[:, bass.ds(n, 1)])
                else:
                    dve.wait_ge(S.turned, n + 1)
                L.finish(dve, G, n, b, acc, xn, xt, z, own[b] if not pre else None)
                if pre:
                    source = L.norm_of(G, n, b)
                    dve.tensor_scalar(z[:, 0:256], source, G.mv_all[:, bass.ds(n * 2, 1)],
                                      G.root_all[:, bass.ds(n, 1)], ALU.subtract, ALU.mult)
                elif L.norm:
                    source = L.norm_of(G, n, b)
                    dve.drain()
                    dve.bn_stats(G.stats[:, :], source)
                    dve.drain()
                    dve.bn_aggr(G.mv[:, :], G.stats[:, :])
                    dve.drain()
                    dve.tensor_scalar(G.mv[:, 1:2], G.mv[:, 1:2], LN_EPS, None, ALU.add)
                    dve.drain().then_inc(S.var, 1)
                    dve.wait_ge(S.dev, n + 1)
                    dve.reciprocal(G.dev2[:, :], G.dev[:, :])
                    dve.drain()
                    dve.tensor_scalar(z[:, 0:256], source, G.mv[:, 0:1], G.dev2[:, :], ALU.subtract, ALU.mult)
                dve.drain().then_inc(S.z, 1)

            if pre:
                with dve.Fori(0, NT) as i:
                    dve.bn_stats(G.stats_all[:, bass.ds(i * 6, 6)], L.norm_of(G, i, 0))
                dve.drain()
                for j in range(NT):
                    dve.bn_aggr(G.mv_all[:, 2 * j:2 * j + 2], G.stats_all[:, 6 * j:6 * j + 6])
                dve.drain()
                dve.tensor_scalar(G.root_all[:, :], G.mv_all[:, :].rearrange("p (n c) -> p n c", c=2)[:, :, 1], LN_EPS,
                                  None, ALU.add)
                dve.drain().then_inc(S.var, 1)
                dve.wait_ge(S.dev, 1)
                dve.reciprocal(G.root_all[:, :], G.root_all[:, :])
                dve.drain()
            walk(dve, agg, post, post if gat else None)

    M.end_phase()


def finish_none(dve, G, n, b, acc, xn, xt, z, own):
    pass


def finish_gat1(dve, G, n, b, acc, xn, xt, z, own):
    for h in range(4):
        c = slice(h * P, (h + 1) * P)
        dve.scalar_tensor_tensor(out=z[:, c], in0=acc[:, c], scalar=G.rden[:, h:h + 1], in1=G.b1[:, c],
                                 op0=ALU.mult, op1=ALU.add)
    dve.drain()
    dve.tensor_scalar(G.neg[:, :], z[:, 0:512], 0.0, G.slope[:, 0:1], ALU.min, ALU.mult)
    dve.drain()
    dve.scalar_tensor_tensor(out=z[:, 0:512], in0=z[:, 0:512], scalar=0.0, in1=G.neg[:, :], op0=ALU.max, op1=ALU.add)


def finish_gat2(dve, G, n, b, acc, xn, xt, z, own):
    dve.scalar_tensor_tensor(out=xn, in0=acc[:, 0:256], scalar=G.rden[:, 0:1], in1=G.b2[:, :],
                             op0=ALU.mult, op1=ALU.add)
    dve.drain()
    dve.tensor_tensor(xn, xn, xt, ALU.add)


def finish_gat3(dve, G, n, b, acc, xn, xt, z, own):
    for h in range(2):
        c = slice(h * P, (h + 1) * P)
        dve.scalar_tensor_tensor(out=xn[:, c], in0=acc[:, c], scalar=G.rden[:, h:h + 1], in1=xt[:, c],
                                 op0=ALU.mult, op1=ALU.add)
    dve.drain()
    for h in range(2):
        c = slice(h * P, (h + 1) * P)
        dve.scalar_tensor_tensor(out=xn[:, c], in0=own[:, c], scalar=G.none[:, h:h + 1], in1=xn[:, c],
                                 op0=ALU.mult, op1=ALU.add)


def finish_gcn1(dve, G, n, b, acc, xn, xt, z, own):
    dve.scalar_tensor_tensor(out=z[:, 0:256], in0=acc[:, 0:256], scalar=G.dinv[:, bass.ds(n, 1)], in1=G.b4[:, :],
                             op0=ALU.mult, op1=ALU.add)
    dve.drain()
    dve.tensor_scalar(z[:, 0:256], z[:, 0:256], 0.0, None, ALU.max)


def finish_gcn2(dve, G, n, b, acc, xn, xt, z, own):
    dve.scalar_tensor_tensor(out=xn, in0=acc[:, 0:256], scalar=G.dinv[:, bass.ds(n, 1)], in1=G.b5[:, :],
                             op0=ALU.mult, op1=ALU.add)
    dve.drain()
    dve.scalar_tensor_tensor(out=xn, in0=xn, scalar=0.0, in1=xt, op0=ALU.max, op1=ALU.add)


def finish_max(dve, G, n, b, acc, xn, xt, z, own):
    dve.tensor_tensor(xn, own, acc[:, 0:256], ALU.add)
    dve.drain()
    dve.scalar_tensor_tensor(out=xn, in0=xn, scalar=0.0, in1=xt, op0=ALU.max, op1=ALU.add)


def inverse_degrees(nc, M, G):
    s1, s2 = M.sem("s_deg"), M.sem("s_root")
    with nc.Block() as block:

        @block.vector
        def _(dve):
            dve.tensor_scalar(G.wroot[:, :], G.wdeg[:, :], 1.2e-35, None, ALU.max)
            dve.drain().then_inc(s1, 1)
            dve.tensor_scalar(G.wdeg[:, :], G.wdeg[:, :], 0.0, None, ALU.is_gt)
            dve.wait_ge(s2, 1)
            dve.reciprocal(G.dinv[:, :], G.dinv[:, :])
            dve.drain()
            dve.tensor_tensor(G.dinv[:, :], G.dinv[:, :], G.wdeg[:, :], ALU.mult)

        @block.scalar
        def _(act):
            act.wait_ge(s1, 1)
            act.activation(G.dinv[:, :], G.wroot[:, :], ACT.Sqrt).then_inc(s2, 1)


def clear_rows(nc, M, G):
    end = G.NT * 256
    half = end // 2
    with nc.Block() as block:

        @block.vector
        def _(dve):
            dve.memset(G.store[:, 0:half], 0.0)

        @block.gpsimd
        def _(pool):
            pool.memset(G.store[:, half:end], 0.0)


def graph_network(nc, a, out):
    with ExitStack() as ctx:
        M = Mem(nc, ctx)
        G = kernel_shapes(a.x.shape[0], a.src.shape[0])
        NT = G.NT
        G.banks = [M.ps(f"bank{j}", [P, 512]) for j in range(8)]
        G.store = M.sb("store", [P, 2 * SLOTS * 520])
        G.work = M.sb("work", [P, 2 * 16 * P])
        top = [0]

        def arena(name, n, dt=F32):
            at, top[0] = top[0], top[0] + n
            assert top[0] <= G.store.shape[1], (name, top[0])
            return G.store[:, at:at + n] if dt is F32 else G.store[:, at:at + n].bitcast(dt)

        G.early = M.sb("early", [P, TILES_AT_ONCE * P])

        constants(nc, M, G)
        G.before = [arena(f"before{k}", G.ET * NT) for k in (IN, OUT)]
        keep = top[0]
        edge_keys(nc, M, G, arena, a.src, a.dst, a.edge_weight)
        top[0] -= 4 * 4 * P
        histograms(nc, M, G, arena)
        top[0] = keep
        node_order(nc, M, G, arena)
        top[0] = keep
        scatter_edges(nc, M, G, arena)
        M.end_phase()
        G.arena_at = NT * 256
        weights(nc, M, G, a)

        G.corr = M.sb("corr", [P, 4 * P])
        G.lst = M.sb("lst", [P, 2, SLOTS, 2], I32)
        G.own = M.sb("own", [P, 2, 520])
        G.acc = M.sb("acc", [P, 2, 512])
        G.xt = M.sb("xt", [P, 2, 256])
        G.xn = M.sb("xn", [P, 2, 256])
        G.z = M.sb("z", [P, 512])
        G.zt = M.sb("zt", [P, 512])
        G.row = M.sb("row", [P, 2, 520])
        G.neg = G.xn[:, :, :].rearrange("p b f -> p (b f)")
        G.logits = M.sb("logits", [P, 4, SLOTS + 1])
        G.probs = M.sb("probs", [P, 4, SLOTS + 1])
        G.mask = M.sb("mask", [P, SLOTS])
        G.mnew = M.sb("mnew", [P, 4])
        G.dsum = M.sb("dsum", [P, 4])
        G.rden = M.sb("rden", [P, 4])
        G.some = M.sb("some", [P, 4])
        G.none = M.sb("none", [P, 4])
        G.stats = M.sb("stats", [P, 6])
        G.mv = M.sb("mv", [P, 2])
        G.dev = M.sb("dev", [P, 1])
        G.dev2 = M.sb("dev2", [P, 1])
        G.wsum = M.sb("wsum", [P, 1])
        G.wpart = M.sb("wpart", [P, 1])
        G.wdeg = M.sb("wdeg", [P, NT])
        G.wroot = M.sb("wroot", [P, NT])
        G.dinv = M.sb("dinv", [P, NT])
        G.m = M.sb("m", [P, 2, 4])
        G.den = M.sb("den", [P, 2, 4])
        G.ids_t = M.sb("ids_t", [P, 2], I32)
        G.mv_all, G.stats_all, G.root_all = G.work[:, 0:2 * NT], G.work[:, 2 * NT:8 * NT], G.work[:, 8 * NT:9 * NT]
        G.part = G.work[:, 0:NGROUP * 256].rearrange("p (g f) -> p g f", f=256)

        T = G.tables

        def of_x(G, n, b):
            return G.x_all[:, bass.ds(n, 1), :].rearrange("p o f -> p (o f)")

        def of_xn(G, n, b):
            return G.xn[:, b, :]

        layer(nc, M, G, Layer("pre", "pre", IN, 1, 256, 0, norm=True, norm_of=of_x, stores=[(T[0][0:G.PAD_ROW], 0, 520)],
                          weight=G.W1, depth=2, out_width=520))
        clear_rows(nc, M, G)
        layer(nc, M, G, Layer("gat1", "gat", IN, 4, 512, 520, table=T[0], own_from=T[0], sum_weights=True,
                          stores=[(T[1][0:G.PAD_ROW], 0, 258)], weight=G.W2, depth=4, out_width=258, finish=finish_gat1))
        inverse_degrees(nc, M, G)
        layer(nc, M, G, Layer("gat2", "gat", IN, 1, 256, 258, table=T[1], own_from=T[1], x_in=G.x[0], x_out=G.x[1],
                          norm=True, norm_of=of_xn, stores=[(T[2][0:G.PAD_ROW], 0, 260)], weight=G.W3,
                          bias_row=G.row3, depth=2, out_width=260, finish=finish_gat2))
        layer(nc, M, G, Layer("gat3", "gat", OUT, 2, 256, 260, table=T[2], own_from=T[2], x_in=G.x[1], x_out=G.x[2],
                          self_loop=False, norm=True, norm_of=of_xn, scale_out=True,
                          stores=[(T[3][0:G.PAD_ROW], 0, 256)], weight=G.W4, depth=2, out_width=256, finish=finish_gat3))
        layer(nc, M, G, Layer("gcn1", "gcn", IN, 1, 256, 256, table=T[3], own_from=T[3], scale_out=True,
                          stores=[(T[4][0:G.PAD_ROW], 0, 256)], weight=G.W5, depth=2, out_width=256, finish=finish_gcn1))
        layer(nc, M, G, Layer("gcn2", "gcn", IN, 1, 256, 256, table=T[4], own_from=T[4], x_in=G.x[2], x_out=G.x[3],
                          norm=True, norm_of=of_xn, stores=[(T[5][0:G.PAD_ROW], 0, 256), (G.own6, 256, 512)],
                          weight=G.W6, bias_row=G.row6, depth=2, out_width=512, finish=finish_gcn2))
        layer(nc, M, G, Layer("edge", "max", IN, 1, 256, 256, table=T[5], own_from=G.own6, x_in=G.x[3],
                          finish=finish_max, out=out))


def kernel(**inputs):
    import concourse.bacc as bacc
    from concourse.bass_utils import run_bass_kernel_spmd as run

    nc = bacc.Bacc("TRN2", target_bir_lowering=False, num_devices=1)
    arrays, aps = {}, {}
    for name, v in inputs.items():
        v = np.ascontiguousarray(v)
        if v.ndim == 0:
            v = v.reshape(1, 1)
        arrays[f"in_{name}"] = v
        aps[name] = nc.dram_tensor(f"in_{name}", v.shape, mybir.dt.from_np(v.dtype), kind="ExternalInput").ap()
    N, D = inputs["x"].shape
    out = nc.dram_tensor("out", (N, D), F32, kind="ExternalOutput").ap()
    a = Named()
    a.x = aps["x"]
    a.src = aps["src"]
    a.dst = aps["dst"]
    a.edge_weight = aps["edge_weight"]
    a.W1 = aps["L0_gnn_W1"]
    a.as1 = aps["L0_gnn_a_src1"]
    a.ad1 = aps["L0_gnn_a_dst1"]
    a.b1 = aps["L0_gnn_b1"]
    a.slope = aps["L0_gnn_prelu_w"]
    a.W2 = aps["L0_gnn_W2"]
    a.as2 = aps["L0_gnn_a_src2"]
    a.ad2 = aps["L0_gnn_a_dst2"]
    a.b2 = aps["L0_gnn_b2"]
    a.W3 = aps["L1_gnn_W_w"]
    a.b3 = aps["L1_gnn_W_b"]
    a.a3 = aps["L1_gnn_a"]
    a.W4 = aps["L2_gnn_W1"]
    a.b4 = aps["L2_gnn_b1"]
    a.W5 = aps["L2_gnn_W2"]
    a.b5 = aps["L2_gnn_b2"]
    a.theta = aps["L3_gnn_theta_w"]
    a.theta_b = aps["L3_gnn_theta_b"]
    a.phi = aps["L3_gnn_phi_w"]
    a.phi_b = aps["L3_gnn_phi_b"]
    graph_network(nc, a, out)
    r = run(nc, [arrays], core_ids=[0])
    return r.results[0]["out"]
```
